# Optimizing a Trainium2 kernel written in Bass

```python
import numpy as np
import jax
import jax.numpy as jnp

def _softmax(x, axis=-1):
    return jax.nn.softmax(x, axis=axis)

def _gelu(x):
    return jax.nn.gelu(x, approximate=True)

def _silu(x):
    return jax.nn.silu(x)

def _sigmoid(x):
    return jax.nn.sigmoid(x)

def _layernorm(x, axis=-1, eps=1e-05):
    m = jnp.mean(x, axis=axis, keepdims=True)
    v = jnp.var(x, axis=axis, keepdims=True)
    return (x - m) / jnp.sqrt(v + eps)

def _scatter_add(tgt, idx, src, axis=0):
    return tgt.at[idx].add(src)

def _segment_sum(src, seg, n):
    return jax.ops.segment_sum(src, seg, n)
kernel_name = 'mk_hybrid_d1_jaxref_r4_fb9d23'

def setup_inputs(seed: int=0):
    np.random.seed(seed)
    _w = jnp.asarray

    def _L0_attn_a_setup():
        import jax, jax.numpy as jnp
        import numpy as np
        import math
        BATCH, L, D_IN, N_STATE, D_OUT = (16, 512, 256, 256, 256)
        INIT_SCALE = 0.5
        CLAMP = 1000000.0
        LN_EPS = 1e-05
        key = jax.random.key(seed)
        ku, ka, kb, kc = jax.random.split(key, 4)
        u = jax.random.normal(ku, (BATCH, L, D_IN), dtype=jnp.float32)
        A_diag = jax.random.normal(ka, (N_STATE,), dtype=jnp.float32) * 0.1
        Bmat = jax.random.normal(kb, (N_STATE, D_IN), dtype=jnp.float32) * (INIT_SCALE / math.sqrt(D_IN))
        Cmat = jax.random.normal(kc, (D_OUT, N_STATE), dtype=jnp.float32) * (INIT_SCALE / math.sqrt(D_IN))
        Dmat = jnp.zeros((D_OUT, D_IN), dtype=jnp.float32)
        h0 = jnp.zeros((N_STATE,), dtype=jnp.float32)
        ln_gamma = jnp.ones((D_OUT,), dtype=jnp.float32)
        ln_beta = jnp.zeros((D_OUT,), dtype=jnp.float32)
        return {'u': u, 'A_diag': A_diag, 'Bmat': Bmat, 'Cmat': Cmat, 'Dmat': Dmat, 'h0': h0, 'ln_gamma': ln_gamma, 'ln_beta': ln_beta}
    _L0_attn_a_in = _L0_attn_a_setup()

    def _L0_attn_b_setup():
        import jax, jax.numpy as jnp
        import numpy as np
        B, T, C = (64, 64, 256)
        N_HEAD, HEAD_SIZE, KV_RANK = (16, 64, 128)
        BLOCK_SIZE = 64
        key = jax.random.key(seed)
        ks = jax.random.split(key, 5)
        HD = N_HEAD * HEAD_SIZE

        def init(k, shape):
            fan_in = shape[0]
            bound = 1.0 / np.sqrt(fan_in)
            return jax.random.uniform(k, shape, jnp.float32, -bound, bound)
        return {'x': jax.random.normal(ks[0], (B, T, C), jnp.float32), 'w_kv_down': init(ks[1], (C, KV_RANK)), 'w_kv_up': init(ks[2], (KV_RANK, 2 * HD)), 'w_q': init(ks[3], (C, HD)), 'w_out': init(ks[4], (HD, C))}
    _L0_attn_b_in = _L0_attn_b_setup()

    def _L0_ffn_setup():
        import jax, jax.numpy as jnp
        import numpy as np
        DIM = 256

        def _reference_tuple_inner(x, W_r, W_k, W_v, mu_r, mu_k):
            B, T, C = x.shape
            x_prev = jnp.concatenate([jnp.zeros((B, 1, C), x.dtype), x[:, :-1, :]], axis=1)
            xr = mu_r * x + (1.0 - mu_r) * x_prev
            xk = mu_k * x + (1.0 - mu_k) * x_prev
            r = jax.nn.sigmoid(jnp.einsum('btc,dc->btd', xr, W_r))
            k = jnp.einsum('btc,dc->btd', xk, W_k)
            k_act = jnp.square(jax.nn.relu(k))
            out = r * jnp.einsum('btc,dc->btd', k_act, W_v)
            new_state = x[:, -1, :]
            return (out, new_state)
        key = jax.random.key(seed)
        ks = jax.random.split(key, 6)
        B, T, C = (8, 512, DIM)
        x = jax.random.normal(ks[0], (B, T, C), dtype=jnp.float32)
        s = 1.0 / np.sqrt(C)
        W_r = jax.random.uniform(ks[1], (C, C), jnp.float32, -s, s)
        W_k = jax.random.uniform(ks[2], (C, C), jnp.float32, -s, s)
        W_v = jax.random.uniform(ks[3], (C, C), jnp.float32, -s, s)
        mu_r = jax.random.uniform(ks[4], (C,), jnp.float32)
        mu_k = jax.random.uniform(ks[5], (C,), jnp.float32)
        return {'x': x, 'W_r': W_r, 'W_k': W_k, 'W_v': W_v, 'mu_r': mu_r, 'mu_k': mu_k}
    _L0_ffn_in = _L0_ffn_setup()
    _d = {'L0_attn_a_u': _L0_attn_a_in['u'], 'L0_attn_a_A_diag': _L0_attn_a_in['A_diag'], 'L0_attn_a_Bmat': _L0_attn_a_in['Bmat'], 'L0_attn_a_Cmat': _L0_attn_a_in['Cmat'], 'L0_attn_a_Dmat': _L0_attn_a_in['Dmat'], 'L0_attn_a_h0': _L0_attn_a_in['h0'], 'L0_attn_a_ln_gamma': _L0_attn_a_in['ln_gamma'], 'L0_attn_a_ln_beta': _L0_attn_a_in['ln_beta'], 'L0_attn_b_w_kv_down': _L0_attn_b_in['w_kv_down'], 'L0_attn_b_w_kv_up': _L0_attn_b_in['w_kv_up'], 'L0_attn_b_w_q': _L0_attn_b_in['w_q'], 'L0_attn_b_w_out': _L0_attn_b_in['w_out'], 'L0_ffn_W_r': _L0_ffn_in['W_r'], 'L0_ffn_W_k': _L0_ffn_in['W_k'], 'L0_ffn_W_v': _L0_ffn_in['W_v'], 'L0_ffn_mu_r': _L0_ffn_in['mu_r'], 'L0_ffn_mu_k': _L0_ffn_in['mu_k']}
    _x0 = _d['L0_attn_a_u']
    _d['L0_attn_a_u'] = jax.random.normal(jax.random.fold_in(jax.random.key(seed), 1), (2, 2048, 256), dtype=_x0.dtype)
    del _x0
    return _d

def reference(L0_attn_a_u, L0_attn_a_A_diag, L0_attn_a_Bmat, L0_attn_a_Cmat, L0_attn_a_Dmat, L0_attn_a_h0, L0_attn_a_ln_gamma, L0_attn_a_ln_beta, L0_attn_b_w_kv_down, L0_attn_b_w_kv_up, L0_attn_b_w_q, L0_attn_b_w_out, L0_ffn_W_r, L0_ffn_W_k, L0_ffn_W_v, L0_ffn_mu_r, L0_ffn_mu_k):

    def _L0_attn_a_ref(u, A_diag, Bmat, Cmat, Dmat, h0, ln_gamma, ln_beta):
        import jax, jax.numpy as jnp
        import numpy as np
        import math
        BATCH, L, D_IN, N_STATE, D_OUT = (16, 512, 256, 256, 256)
        INIT_SCALE = 0.5
        CLAMP = 1000000.0
        LN_EPS = 1e-05
        a = -jax.nn.softplus(A_diag)
        bu = jnp.einsum('bld,nd->lbn', u, Bmat)

        def step(x, bu_t):
            x = a * x + bu_t
            return (x, x)
        x_init = jnp.broadcast_to(h0, (u.shape[0], h0.shape[0]))
        _, xs = jax.lax.scan(step, x_init, bu)
        y = jnp.einsum('lbn,on->blo', xs, Cmat) + jnp.einsum('bld,od->blo', u, Dmat)
        act = jax.nn.gelu(y, approximate=False)
        mean = jnp.mean(act, axis=-1, keepdims=True)
        var = jnp.var(act, axis=-1, keepdims=True)
        normed = (act - mean) * jax.lax.rsqrt(var + LN_EPS) * ln_gamma + ln_beta
        return jnp.nan_to_num(normed, nan=0.0, posinf=CLAMP, neginf=-CLAMP)

    def _L0_attn_b_ref(x, w_kv_down, w_kv_up, w_q, w_out):
        import jax, jax.numpy as jnp
        import numpy as np
        B, T, C = (64, 64, 256)
        N_HEAD, HEAD_SIZE, KV_RANK = (16, 64, 128)
        BLOCK_SIZE = 64
        Bx, Tx, Cx = x.shape
        HD = N_HEAD * HEAD_SIZE
        latent_kv = x @ w_kv_down
        kv = latent_kv @ w_kv_up
        k, v = (kv[..., :HD], kv[..., HD:])
        k = k.reshape(Bx, Tx, N_HEAD, HEAD_SIZE)
        v = v.reshape(Bx, Tx, N_HEAD, HEAD_SIZE)
        q = (x @ w_q).reshape(Bx, Tx, N_HEAD, HEAD_SIZE)
        scale = HEAD_SIZE ** (-0.5)
        att = jnp.einsum('bqhd,bkhd->bhqk', q, k) * scale
        causal = jnp.tril(jnp.ones((Tx, Tx), dtype=bool))
        att = jnp.where(causal, att, -jnp.inf)
        att = jax.nn.softmax(att, axis=-1)
        y = jnp.einsum('bhqk,bkhd->bqhd', att, v)
        y = y.reshape(Bx, Tx, HD)
        return y @ w_out

    def _L0_ffn_ref(x, W_r, W_k, W_v, mu_r, mu_k):
        import jax, jax.numpy as jnp
        import numpy as np
        DIM = 256

        def _reference_tuple_inner(x, W_r, W_k, W_v, mu_r, mu_k):
            B, T, C = x.shape
            x_prev = jnp.concatenate([jnp.zeros((B, 1, C), x.dtype), x[:, :-1, :]], axis=1)
            xr = mu_r * x + (1.0 - mu_r) * x_prev
            xk = mu_k * x + (1.0 - mu_k) * x_prev
            r = jax.nn.sigmoid(jnp.einsum('btc,dc->btd', xr, W_r))
            k = jnp.einsum('btc,dc->btd', xk, W_k)
            k_act = jnp.square(jax.nn.relu(k))
            out = r * jnp.einsum('btc,dc->btd', k_act, W_v)
            new_state = x[:, -1, :]
            return (out, new_state)
        return _reference_tuple_inner(x, W_r, W_k, W_v, mu_r, mu_k)[0]
    x = L0_attn_a_u
    x = x + _L0_attn_a_ref(_layernorm(x, axis=-1), L0_attn_a_A_diag, L0_attn_a_Bmat, L0_attn_a_Cmat, L0_attn_a_Dmat, L0_attn_a_h0, L0_attn_a_ln_gamma, L0_attn_a_ln_beta)
    x = x + _L0_ffn_ref(_layernorm(x, axis=-1), L0_ffn_W_r, L0_ffn_W_k, L0_ffn_W_v, L0_ffn_mu_r, L0_ffn_mu_k)
    x = x + _L0_attn_b_ref(_layernorm(x, axis=-1), L0_attn_b_w_kv_down, L0_attn_b_w_kv_up, L0_attn_b_w_q, L0_attn_b_w_out)
    x = x + _L0_ffn_ref(_layernorm(x, axis=-1), L0_ffn_W_r, L0_ffn_W_k, L0_ffn_W_v, L0_ffn_mu_r, L0_ffn_mu_k)
    return x

_drawn_inputs = setup_inputs


def setup_inputs(seed=0):
    import zlib

    import numpy as np

    out = dict(_drawn_inputs(seed))
    spreads = {'L0_attn_a_Dmat': (0.0, 0.1),
     'L0_attn_a_h0': (0.0, 0.8),
     'L0_attn_a_ln_gamma': (1.0, 0.2),
     'L0_attn_a_ln_beta': (0.0, 0.1)}
    factors = {'L0_attn_b_w_kv_down': 3.969,
     'L0_attn_b_w_kv_up': 4.249,
     'L0_attn_b_w_q': 8.0,
     'L0_attn_b_w_out': 4.303,
     'L0_ffn_mu_r': 4.636}
    for name, (base, spread) in spreads.items():
        noise = np.random.default_rng([zlib.crc32(name.encode()), seed]).standard_normal(out[name].shape)
        drawn = base * np.exp(spread * noise) if base else spread * noise
        out[name] = jnp.asarray(drawn.astype(out[name].dtype))
    for name, factor in factors.items():
        out[name] = (out[name] * factor).astype(out[name].dtype)
    return out
```

```python
from contextlib import ExitStack

import concourse.bass as bass
from concourse import mybir

ALU = mybir.AluOpType
ACT = mybir.ActivationFunctionType
AX = mybir.AxisListType
F32 = mybir.dt.float32
F32R = mybir.dt.float32r
BF16 = mybir.dt.bfloat16

P = 128
NB, T, C = 2, 2048, 256
CH = C // P
BLK = 512
NBLK = T // BLK
TPB = BLK // P
NT = T // P
NH, DH = 16, 64
NPAIR = NH // 2
RANK = 128
EPS = 1e-5
CLAMP = 1e6
MASKED = -3.0e38
WPC = 2 * P + P + P + C
NK = NBLK + 1


class Program:

    def __init__(self, nc, ctx):
        self.nc, self.ctx = nc, ctx
        self.engine = {"tensor": nc.tensor, "vector": nc.vector, "scalar": nc.scalar,
                       "gpsimd": nc.gpsimd, "sync": nc.sync}
        self.sems, self.value, self.waited = {}, {}, {}

    def do(self, engine, step, make):
        return self._signal(engine, step, make, 1)

    def dma(self, step, out, in_):
        return self._signal("sync", step, lambda e: e.dma_start(out, in_), 16)

    def _signal(self, engine, step, make, by):
        if step not in self.sems:
            self.sems[step] = self.ctx.enter_context(self.nc.semaphore(step))
            self.value[step] = 0
        self.value[step] += by
        sem = self.sems[step]
        make(self.engine[engine]).then_inc(sem, by)
        return step, self.value[step]

    def run(self, engine, make):
        make(self.engine[engine])

    def need(self, engine, *done):
        for d in done:
            if d is None:
                continue
            if isinstance(d, list):
                self.need(engine, *d)
                continue
            step, value = d
            if self.waited.get((engine, step), 0) < value:
                self.waited[engine, step] = value
                self.engine[engine].wait_ge(self.sems[step], value)

    def everything_so_far(self):
        return [(s, v) for s, v in self.value.items()]


def build(nc, u, wA, wF, wKD, wPair, aDiag, h0, gb, mu, out):
    ctx = ExitStack()
    with ctx:
        pg = Program(nc, ctx)
        do, dma, run, need = pg.do, pg.dma, pg.run, pg.need

        def sb(where, name, shape, dt=F32):
            return where.enter_context(nc.sbuf_tensor(name, shape, dt))

        scores = [ctx.enter_context(nc.psum_tensor(f"scores{i}", [P, 2, BLK], F32)) for i in range(2)]
        heads_out = [ctx.enter_context(nc.psum_tensor(f"heads_out{i}", [P, BLK], F32)) for i in range(2)]
        work = [ctx.enter_context(nc.psum_tensor(f"work{i}", [P, BLK], F32)) for i in range(2)]
        wide = [work[0][:, :], work[1][:, :], scores[0][:, 0, :], scores[0][:, 1, :],
                scores[1][:, 0, :], scores[1][:, 1, :], heads_out[0][:, :], heads_out[1][:, :]]
        bank_free = {}
        turn = {"next": 0, "banks": 8}

        def bank():
            n = turn["next"] % turn["banks"]
            turn["next"] += 1
            need("tensor", bank_free.get(n))
            return n, wide[n]

        X = sb(ctx, "X", [P, NB * NT, C])
        ident = sb(ctx, "ident", [P, P])
        ident16 = sb(ctx, "ident16", [P, P], BF16)
        mean_var = sb(ctx, "mean_var", [P, NB * NT, 2])
        stats = sb(ctx, "stats", [P, 4, 6])
        std = sb(ctx, "std", [P, NB * NT])
        rstd = sb(ctx, "rstd", [P, NB * NT])

        x_in = []
        for b in range(NB):
            for j in range(NBLK):
                k = (b * NBLK + j)
                x_in.append(dma(f"x_in{k}", X[:, k * TPB:(k + 1) * TPB, :],
                                u[k * BLK:(k + 1) * BLK, :].rearrange("(t p) c -> p t c", p=P)))
        X_done = {k: [x_in[k // TPB]] for k in range(NB * NT)}

        z = [do("gpsimd", "ident_zero", lambda e: e.memset(ident[:, :], 0.0)),
             do("gpsimd", "ident_zero", lambda e: e.memset(ident16[:, :], 0.0))]
        need("gpsimd", z)
        for m in (ident, ident16):
            ident_ok = do("gpsimd", "ident", lambda e, m=m: e.affine_select(
                out=m[:, :], in_=m[:, :], compare_op=ALU.not_equal, fill=1.0, base=0,
                pattern=[[-1, P]], channel_multiplier=1))

        stats_free = [None] * 4

        def layer_stats(tiles, source, ready):
            for n, k in enumerate(tiles):
                s = n % 4
                need("vector", ready(k), stats_free[s], norm_free)
                t = do("vector", "bn_stats", lambda e, k=k, s=s: e.bn_stats(stats[:, s, :], source(k)))
                need("vector", t)
                stats_free[s] = do("vector", "bn_aggr", lambda e, k=k, s=s: e.bn_aggr(
                    mean_var[:, k, :], stats[:, s, :]))
            a, z = tiles[0], tiles[-1] + 1
            need("vector", stats_free[(len(tiles) - 1) % 4])
            t = do("vector", "var_eps", lambda e: e.tensor_scalar(std[:, a:z], mean_var[:, a:z, 1], EPS, None, ALU.add))
            need("scalar", t)
            t = do("scalar", "std", lambda e: e.activation(std[:, a:z], std[:, a:z], ACT.Sqrt))
            need("vector", t)
            return do("vector", "rstd", lambda e: e.reciprocal(rstd[:, a:z], std[:, a:z]))

        norm_free = None

        def normalise(engine, dst, src, k, step):
            return do(engine, step, lambda e: e.tensor_scalar(
                dst, src, mean_var[:, k, 0:1], rstd[:, k:k + 1], ALU.subtract, ALU.mult))

        def terms(a, b):
            return [(a[0], b[0]), (a[0], b[1]), (a[1], b[0])]

        def product(dst, pairs, first=True, last=True):
            made = []
            for n, (l, r) in enumerate(pairs):
                made.append(lambda e, l=l, r=r, s=(first and n == 0), z=(last and n == len(pairs) - 1):
                            e.matmul(dst, l, r, start=s, stop=z))
            for m in made[:-1]:
                run("tensor", m)
            return made[-1]

        def split_weights(name, raw, hi, lo, src, free=None):
            need("sync", free)
            t = dma(f"{name}_in", raw, src)
            need("vector", t, free)
            t = do("vector", f"{name}_hi", lambda e: e.tensor_copy(hi, raw))
            need("vector", t)
            return do("vector", f"{name}_lo", lambda e: e.tensor_tensor(lo, raw, hi, ALU.subtract))

        def transposed_tiles(k0, xn_of, ready):
            res = []
            for h in range(CH):
                n, ps = bank()
                for t in range(TPB):
                    need("tensor", ready[t], ident_ok)
                    f = lambda e, t=t, h=h, ps=ps: e.transpose(
                        ps[:, t * P:(t + 1) * P], xn_of(t)[:, h * P:(h + 1) * P], ident[:, :])
                    if t < TPB - 1:
                        run("tensor", f)
                done = do("tensor", "x_turned", f)
                res.append((n, ps, done))
            return res

        with ExitStack() as ph:
            w_raw = sb(ph, "wA_raw", [P, 3, CH, C])
            w_hi = sb(ph, "wA_hi", [P, 3, CH, C], F32R)
            w_lo = sb(ph, "wA_lo", [P, 3, CH, C], F32R)
            a_in = sb(ph, "a_in", [P, CH])
            a_abs = sb(ph, "a_abs", [P, CH])
            a_log = sb(ph, "a_log", [P, CH])
            a_col = sb(ph, "a_col", [P, CH])
            zeros = sb(ph, "zeros", [P, BLK])
            decay = sb(ph, "decay", [P, CH, BLK])
            state0 = sb(ph, "state0", [P, CH])
            gamma_beta = sb(ph, "gamma_beta", [P, 2, C])
            xn = sb(ph, "xn", [P, 2, TPB, C])
            xT_hi = sb(ph, "xT_hi", [P, 2, CH, BLK], F32R)
            xT_lo = sb(ph, "xT_lo", [P, 2, CH, BLK], F32R)
            xs = sb(ph, "xs", [P, 2, CH, BLK])
            xs_hi = sb(ph, "xs_hi", [P, 2, CH, BLK], F32R)
            xs_lo = sb(ph, "xs_lo", [P, 2, CH, BLK], F32R)
            G = sb(ph, "G", [P, NT, C])
            nrm = sb(ph, "nrm", [P, 2, C])
            clp = sb(ph, "clp", [P, 2, C])
            msk = sb(ph, "msk", [P, 2, C])
            fin = sb(ph, "fin", [P, 2, C], mybir.dt.uint32)

            small_in = dma("ssm_small_in", a_in[:, :], aDiag)
            small_in = dma("ssm_small_in", state0[:, :], h0)
            small_in = dma("ssm_small_in", gamma_beta[:, :, :], gb)
            wA_ok = split_weights("wA", w_raw[:, :, :, :], w_hi[:, :, :, :], w_lo[:, :, :, :], wA)
            zeros_ok = do("vector", "zeros", lambda e: e.memset(zeros[:, :], 0.0))
            need("vector", small_in)
            t = do("vector", "softplus_v", lambda e: e.tensor_scalar(a_abs[:, :], a_in[:, :], -1.0, None, ALU.mult))
            need("vector", t)
            t = do("vector", "softplus_v", lambda e: e.tensor_tensor(a_abs[:, :], a_abs[:, :], a_in[:, :], ALU.min))
            need("scalar", t)
            t = do("scalar", "softplus_a", lambda e: e.activation(a_log[:, :], a_abs[:, :], ACT.Exp))
            need("scalar", t)
            t = do("scalar", "softplus_a", lambda e: e.activation(a_log[:, :], a_log[:, :], ACT.Ln, bias=1.0))
            need("vector", t)
            t = do("vector", "softplus_v", lambda e: e.scalar_tensor_tensor(
                out=a_col[:, :], in0=a_in[:, :], scalar=0.0, in1=a_log[:, :], op0=ALU.max, op1=ALU.add))
            need("vector", t, zeros_ok)
            for h in range(CH):
                decay_ok = do("vector", "decay", lambda e, h=h: e.tensor_scalar(
                    decay[:, h, :], zeros[:, :], a_col[:, h:h + 1], None, ALU.subtract))

            def part(m, which):
                return (which[0][:, m], which[1][:, m])

            xn_free, xT_free = [None, None], [None, None]
            xs_free = [None, None]
            scanned = {}
            for b in range(NB):
                rstd_ok = layer_stats(range(b * NT, (b + 1) * NT), lambda k: X[:, k, :], lambda k: X_done[k])
                G_done = {}
                for j in range(NBLK):
                    s = j % 2
                    k0 = b * NT + j * TPB
                    need("vector", rstd_ok, xn_free[s])
                    ready = [normalise("vector", xn[:, s, t, :], X[:, k0 + t, :], k0 + t, "ssm_xn") for t in range(TPB)]
                    turned = transposed_tiles(k0, lambda t, s=s: xn[:, s, t, :], ready)
                    xn_free[s] = turned[-1][2]
                    for h, (n, ps, done) in enumerate(turned):
                        need("scalar", done, xT_free[s])
                        hi = do("scalar", "ssm_xT_hi", lambda e, h=h, s=s, ps=ps: e.activation(xT_hi[:, s, h, :], ps, ACT.Copy))
                        need("vector", hi, done)
                        xT_ok = do("vector", "ssm_xT_lo", lambda e, h=h, s=s, ps=ps: e.tensor_tensor(
                            xT_lo[:, s, h, :], ps, xT_hi[:, s, h, :], ALU.subtract))
                        bank_free[n] = [hi, xT_ok]
                    need("tensor", xT_ok, wA_ok)
                    for m in range(CH):
                        n, ps = bank()
                        pairs = []
                        for c in range(CH):
                            pairs += terms((w_hi[:, 0, c, m * P:(m + 1) * P], w_lo[:, 0, c, m * P:(m + 1) * P]),
                                           (xT_hi[:, s, c, :], xT_lo[:, s, c, :]))
                        bu = do("tensor", "bu", product(ps, pairs))
                        need("vector", bu, decay_ok, small_in, scanned.get((b, j - 1, m)), xs_free[s])
                        init = state0[:, m:m + 1] if j == 0 else xs[:, 1 - s, m, BLK - 1:BLK]
                        sc = do("vector", "scan", lambda e, m=m, s=s, ps=ps, init=init: e.tensor_tensor_scan(
                            xs[:, s, m, :], decay[:, m, :], ps, init, ALU.mult, ALU.add))
                        scanned[b, j, m] = sc
                        bank_free[n] = [sc]
                        need("scalar", sc, xs_free[s])
                        hi = do("scalar", "xs_hi", lambda e, m=m, s=s: e.activation(xs_hi[:, s, m, :], xs[:, s, m, :], ACT.Copy))
                        need("gpsimd", hi, sc, xs_free[s])
                        xs_ok = do("gpsimd", "xs_lo", lambda e, m=m, s=s: e.tensor_tensor(
                            xs_lo[:, s, m, :], xs[:, s, m, :], xs_hi[:, s, m, :], ALU.subtract))
                    need("tensor", xs_ok)
                    for t in range(0, TPB, 2):
                        n, ps = bank()
                        for q in range(2):
                            cols = slice((t + q) * P, (t + q + 1) * P)
                            pairs = []
                            for c in range(CH):
                                pairs += terms((xs_hi[:, s, c, cols], xs_lo[:, s, c, cols]),
                                               (w_hi[:, 1, c, :], w_lo[:, 1, c, :]))
                                pairs += terms((xT_hi[:, s, c, cols], xT_lo[:, s, c, cols]),
                                               (w_hi[:, 2, c, :], w_lo[:, 2, c, :]))
                            y = do("tensor", "ssm_y", product(ps[:, q * C:(q + 1) * C], pairs))
                        kk = j * TPB + t
                        need("scalar", y, norm_free)
                        g = do("scalar", "gelu", lambda e, kk=kk, ps=ps: e.activation(
                            G[:, kk:kk + 2, :], ps.rearrange("p (t c) -> p t c", c=C), ACT.Gelu))
                        bank_free[n] = [g]
                        G_done[kk] = G_done[kk + 1] = g
                    xT_free[s] = y
                    xs_free[s] = [y, xs_ok]
                norm_free = rstd_ok
                rstd_ok = layer_stats(range(b * NT, (b + 1) * NT), lambda k, b=b: G[:, k - b * NT, :],
                                      lambda k, b=b: [G_done[k - b * NT], xn_free[0], xn_free[1], norm_free])
                nrm_free, tail_free = [None, None], [None, None]
                for kk in range(NT):
                    s, k = kk % 2, b * NT + kk
                    need("vector", rstd_ok, nrm_free[s])
                    t = normalise("vector", nrm[:, s, :], G[:, kk, :], k, "act_norm")
                    norm_free = t
                    need("gpsimd", t, small_in)
                    t = do("gpsimd", "act_gamma", lambda e, s=s: e.tensor_tensor(nrm[:, s, :], nrm[:, s, :], gamma_beta[:, 0, :], ALU.mult))
                    need("gpsimd", t)
                    v = do("gpsimd", "act_beta", lambda e, s=s: e.tensor_tensor(nrm[:, s, :], nrm[:, s, :], gamma_beta[:, 1, :], ALU.add))
                    need("vector", v, tail_free[s])
                    t = do("vector", "clamp", lambda e, s=s: e.tensor_scalar(clp[:, s, :], nrm[:, s, :], -CLAMP, CLAMP, ALU.max, ALU.min))
                    m = do("vector", "not_nan", lambda e, s=s: e.tensor_tensor(msk[:, s, :], nrm[:, s, :], nrm[:, s, :], ALU.is_equal))
                    f = do("vector", "is_finite", lambda e, s=s: e.tensor_scalar(fin[:, s, :], nrm[:, s, :], 0.0, 0.0, ALU.mult, ALU.is_equal))
                    need("vector", t, m)
                    t = do("vector", "no_nan", lambda e, s=s: e.tensor_tensor(clp[:, s, :], clp[:, s, :], msk[:, s, :], ALU.mult))
                    need("vector", t, f)
                    t = do("vector", "nan_to_num", lambda e, s=s: e.copy_predicated(clp[:, s, :], fin[:, s, :], nrm[:, s, :]))
                    nrm_free[s] = t
                    need("gpsimd", t)
                    X_done[k] = [do("gpsimd", "x_plus_ssm", lambda e, k=k, s=s: e.tensor_tensor(X[:, k, :], X[:, k, :], clp[:, s, :], ALU.add))]
                    tail_free[s] = X_done[k]

        def channel_mixer(tag, store):
            nonlocal norm_free
            before = pg.everything_so_far()
            turn["banks"] = 8
            with ExitStack() as ph:
                w_raw = sb(ph, f"wF_raw{tag}", [P, 3, CH, C])
                w_hi = sb(ph, f"wF_hi{tag}", [P, 3, CH, C], F32R)
                w_lo = sb(ph, f"wF_lo{tag}", [P, 3, CH, C], F32R)
                mu_sb = sb(ph, f"mu{tag}", [P, 2, CH])
                one_mu = sb(ph, f"one_mu{tag}", [P, 2, CH])
                xn = sb(ph, f"xnF{tag}", [P, 2, TPB, C])
                xT = sb(ph, f"xTF{tag}", [P, 2, CH, BLK + 1])
                old = sb(ph, f"old{tag}", [P, 2, CH, BLK])
                mix = sb(ph, f"mix{tag}", [P, 2, CH, BLK])
                mix_hi = sb(ph, f"mix_hi{tag}", [P, 2, 2, CH, BLK], F32R)
                mix_lo = sb(ph, f"mix_lo{tag}", [P, 2, 2, CH, BLK], F32R)
                relu = sb(ph, f"relu{tag}", [P, 2, CH, BLK])
                kact = sb(ph, f"kact{tag}", [P, 2, CH, BLK])
                kact_hi = sb(ph, f"kact_hi{tag}", [P, 2, CH, BLK], F32R)
                kact_lo = sb(ph, f"kact_lo{tag}", [P, 2, CH, BLK], F32R)
                gate = sb(ph, f"gate{tag}", [P, 2, TPB, C])
                upd = sb(ph, f"upd{tag}", [P, 2, TPB, C])
                for e in ("sync", "vector", "scalar", "gpsimd"):
                    need(e, before)
                need("sync", before)
                mu_in = dma("mu_in", mu_sb[:, :, :], mu)
                w_ok = split_weights("wF", w_raw[:, :, :, :], w_hi[:, :, :, :], w_lo[:, :, :, :], wF)
                need("vector", mu_in)
                mu_ok = do("vector", "one_minus_mu", lambda e: e.tensor_scalar(one_mu[:, :, :], mu_sb[:, :, :], -1.0, 1.0, ALU.mult, ALU.add))
                xn_free, xT_free, mix_free, kact_free, gate_free, relu_free = ([None, None] for _ in range(6))
                mixf = [None, None]
                stored = []
                rstd_ok = [layer_stats(range(b * NT, (b + 1) * NT), lambda k: X[:, k, :], lambda k: X_done[k]) for b in range(NB)]

                def front(i):
                    b, j = divmod(i, NBLK)
                    s, k0 = i % 2, i * TPB
                    need("vector", rstd_ok[b], xn_free[s])
                    ready = [normalise("vector", xn[:, s, t, :], X[:, k0 + t, :], k0 + t, "ffn_xn") for t in range(TPB)]
                    turned = transposed_tiles(k0, lambda t: xn[:, s, t, :], ready)
                    xn_free[s] = turned[-1][2]
                    if j == 0:
                        need("vector", xT_free[s])
                        edge = do("vector", "ffn_edge", lambda e: e.memset(xT[:, s, :, 0:1], 0.0))
                    else:
                        need("vector", xT_free[s], xT_state["ok"])
                        edge = do("vector", "ffn_edge", lambda e: e.tensor_copy(xT[:, s, :, 0:1], xT[:, 1 - s, :, BLK:BLK + 1]))
                    oks = []
                    for h, (n, ps, done) in enumerate(turned):
                        need("scalar", done, xT_free[s])
                        t = do("scalar", "ffn_xT", lambda e, h=h, ps=ps: e.activation(xT[:, s, h, 1:BLK + 1], ps, ACT.Copy))
                        bank_free[n] = [t]
                        oks.append(t)
                    xT_state["ok"] = oks[-1]
                    for r in range(2):
                        for h in range(CH):
                            need("vector", oks[h], edge, mu_ok, mixf[h])
                            t = do("vector", "mix_old", lambda e, r=r, h=h: e.tensor_scalar(
                                old[:, 0, h, :], xT[:, s, h, 0:BLK], one_mu[:, r, h:h + 1], None, ALU.mult))
                            need("vector", t)
                            t = do("vector", "mix", lambda e, r=r, h=h: e.scalar_tensor_tensor(
                                out=mix[:, 0, h, :], in0=xT[:, s, h, 1:BLK + 1], scalar=mu_sb[:, r, h:h + 1],
                                in1=old[:, 0, h, :], op0=ALU.mult, op1=ALU.add))
                            xT_free[s] = t
                            need("scalar", t, mix_free[s])
                            hi = do("scalar", "mix_hi", lambda e, r=r, h=h: e.activation(mix_hi[:, s, r, h, :], mix[:, 0, h, :], ACT.Copy))
                            need("gpsimd", hi, t, mix_free[s])
                            lo = do("gpsimd", "mix_lo", lambda e, r=r, h=h: e.tensor_tensor(
                                mix_lo[:, s, r, h, :], mix[:, 0, h, :], mix_hi[:, s, r, h, :], ALU.subtract))
                            mixf[h] = lo
                    xT_free[s] = [xT_free[s], edge_reader(i)]
                    mixed[i] = lo

                def edge_reader(i):
                    return None

                xT_state, mixed = {"ok": None}, {}

                def back(i):
                    s, k0 = i % 2, i * TPB
                    need("tensor", mixed[i], w_ok)
                    for m in range(CH):
                        n, ps = bank()
                        pairs = []
                        for c in range(CH):
                            pairs += terms((w_hi[:, 1, c, m * P:(m + 1) * P], w_lo[:, 1, c, m * P:(m + 1) * P]),
                                           (mix_hi[:, s, 1, c, :], mix_lo[:, s, 1, c, :]))
                        t = do("tensor", "ffn_k", product(ps, pairs))
                        need("scalar", t, relu_free[m])
                        t = do("scalar", "ffn_relu", lambda e, m=m, ps=ps: e.activation(relu[:, 0, m, :], ps, ACT.Relu))
                        bank_free[n] = [t]
                        need("vector", t, relu_free[m])
                        t = do("vector", "ffn_square", lambda e, m=m: e.tensor_tensor(kact[:, 0, m, :], relu[:, 0, m, :], relu[:, 0, m, :], ALU.mult))
                        need("vector", t, kact_free[s])
                        hi = do("vector", "kact_hi", lambda e, m=m: e.tensor_copy(kact_hi[:, s, m, :], kact[:, 0, m, :]))
                        need("vector", hi)
                        k_ok = do("vector", "kact_lo", lambda e, m=m: e.tensor_tensor(kact_lo[:, s, m, :], kact[:, 0, m, :], kact_hi[:, s, m, :], ALU.subtract))
                        relu_free[m] = k_ok
                    for t0 in range(0, TPB, 2):
                        n, ps = bank()
                        for q in range(2):
                            cols = slice((t0 + q) * P, (t0 + q + 1) * P)
                            pairs = []
                            for c in range(CH):
                                pairs += terms((mix_hi[:, s, 0, c, cols], mix_lo[:, s, 0, c, cols]),
                                               (w_hi[:, 0, c, :], w_lo[:, 0, c, :]))
                            t = do("tensor", "ffn_r", product(ps[:, q * C:(q + 1) * C], pairs))
                        need("scalar", t, gate_free[s])
                        g_ok = do("scalar", "sigmoid", lambda e, t0=t0, ps=ps: e.activation(
                            gate[:, s, t0:t0 + 2, :], ps.rearrange("p (t c) -> p t c", c=C), ACT.Sigmoid))
                        bank_free[n] = [g_ok]
                    mix_free[s] = t
                    need("tensor", k_ok)
                    for t0 in range(0, TPB, 2):
                        n, ps = bank()
                        for q in range(2):
                            cols = slice((t0 + q) * P, (t0 + q + 1) * P)
                            pairs = []
                            for c in range(CH):
                                pairs += terms((kact_hi[:, s, c, cols], kact_lo[:, s, c, cols]),
                                               (w_hi[:, 2, c, :], w_lo[:, 2, c, :]))
                            t = do("tensor", "ffn_v", product(ps[:, q * C:(q + 1) * C], pairs))
                        need("vector", t, g_ok, gate_free[s])
                        t2 = do("vector", "gated", lambda e, t0=t0, ps=ps: e.tensor_tensor(
                            upd[:, s, t0:t0 + 2, :], ps.rearrange("p (t c) -> p t c", c=C), gate[:, s, t0:t0 + 2, :], ALU.mult))
                        bank_free[n] = [t2]
                        need("gpsimd", t2)
                        k = k0 + t0
                        X_done[k] = X_done[k + 1] = [do("gpsimd", "x_plus_ffn", lambda e, k=k, t0=t0: e.tensor_tensor(
                            X[:, k:k + 2, :], X[:, k:k + 2, :], upd[:, s, t0:t0 + 2, :], ALU.add))]
                    kact_free[s] = t
                    gate_free[s] = X_done[k]
                    if store:
                        need("sync", X_done[k0], X_done[k0 + TPB - 1])
                        stored.append(dma("stored", out[i * BLK:(i + 1) * BLK, :].rearrange("(t p) c -> p t c", p=P),
                                          X[:, k0:k0 + TPB, :]))

                front(0)
                for i in range(NB * NBLK):
                    if i + 1 < NB * NBLK:
                        front(i + 1)
                    back(i)
                if store:
                    need("sync", stored[-1])

        channel_mixer("a", False)

        before = pg.everything_so_far()
        with ExitStack() as ph:
            xT_hi = sb(ph, "att_xT_hi", [P, CH, T], F32R)
            xT_lo = sb(ph, "att_xT_lo", [P, CH, T], F32R)
            lat_hi = sb(ph, "lat_hi", [P, T], F32R)
            lat_lo = sb(ph, "lat_lo", [P, T], F32R)
            kd_raw = sb(ph, "kd_raw", [P, CH, RANK])
            kd_hi = sb(ph, "kd_hi", [P, CH, RANK], F32R)
            kd_lo = sb(ph, "kd_lo", [P, CH, RANK], F32R)
            w_raw = sb(ph, "wP_raw", [P, WPC])
            w_hi = [sb(ph, f"wP_hi{i}", [P, WPC], F32R) for i in range(2)]
            w_lo = [sb(ph, f"wP_lo{i}", [P, WPC], F32R) for i in range(2)]
            qA = [[sb(ph, f"qA{i}{h}", [P, BLK], F32R) for h in range(2)] for i in range(2)]
            qB = [[sb(ph, f"qB{i}{h}", [DH + 4, BLK], F32R) for h in range(2)] for i in range(2)]
            kA = [[sb(ph, f"kA{i}{h}", [P, BLK], F32R) for h in range(2)] for i in range(NK)]
            kB = [[sb(ph, f"kB{i}{h}", [DH + 4, BLK], F32R) for h in range(2)] for i in range(NK)]
            V = [sb(ph, f"V{i}", [P, TPB, P]) for i in range(NK)]
            NP_ = 3
            prob = [sb(ph, f"prob{i}", [P, 2, BLK]) for i in range(NP_)]
            accG = sb(ph, "accG", [P, 2, BLK])
            accV = sb(ph, "accV", [P, 2, BLK])
            ones = sb(ph, "ones", [P, DH])
            sel = sb(ph, "sel", [P, 2, BLK])
            maskQ = sb(ph, "maskQ", [P, P], BF16)
            maskK = sb(ph, "maskK", [P, P], BF16)
            part_max = sb(ph, "part_max", [P, 2 * TPB, NBLK])
            row_max = sb(ph, "row_max", [P, 2 * TPB])
            neg_r = sb(ph, "neg_r", [P, 2 * TPB], F32R)
            neg = sb(ph, "neg", [P, TPB, 2, 2])
            rden = sb(ph, "rden", [P, BLK])
            oT = sb(ph, "oT", [P, BLK])
            oT_hi = sb(ph, "oT_hi", [P, BLK], F32R)
            oT_lo = sb(ph, "oT_lo", [P, BLK], F32R)
            for e in ("sync", "vector", "scalar", "gpsimd"):
                need(e, before)
            turn["banks"] = 2
            kd_ok = split_weights("kd", kd_raw[:, :, :], kd_hi[:, :, :], kd_lo[:, :, :], wKD)
            t = [do("gpsimd", "att_fill", lambda e: e.memset(ones[:, :], 1.0)),
                 do("gpsimd", "att_fill", lambda e: e.memset(sel[:, :, :], 1.0)),
                 do("gpsimd", "att_fill", lambda e: e.memset(maskQ[:, :], 0.0)),
                 do("gpsimd", "att_fill", lambda e: e.memset(maskK[:, :], 0.0))]
            need("gpsimd", t)
            do("gpsimd", "att_const", lambda e: e.affine_select(
                out=sel[:, 0, :], in_=sel[:, 0, :], compare_op=ALU.is_ge, fill=0.0, base=DH + 1,
                pattern=[[0, BLK]], channel_multiplier=-1))
            do("gpsimd", "att_const", lambda e: e.affine_select(
                out=sel[:, 1, :], in_=sel[:, 1, :], compare_op=ALU.is_ge, fill=0.0, base=-(DH + 2),
                pattern=[[0, BLK]], channel_multiplier=1))
            do("gpsimd", "att_const", lambda e: e.affine_select(
                out=maskQ[:, :], in_=maskQ[:, :], compare_op=ALU.is_ge, fill=MASKED, base=0,
                pattern=[[-1, P]], channel_multiplier=1))
            const_ok = do("gpsimd", "att_const", lambda e: e.affine_select(
                out=maskK[:, :], in_=maskK[:, :], compare_op=ALU.is_ge, fill=MASKED, base=0,
                pattern=[[1, P]], channel_multiplier=-1))
            need("vector", const_ok)
            for i in range(NK):
                for h in range(2):
                    sel_ok = do("vector", "sel_rows", lambda e, i=i, h=h: e.tensor_copy(
                        kB[i][h][DH:DH + 4, :], sel[DH:DH + 4, h, :]))
            ones_ok = const_ok

            w_ok, w_free = {}, [None, None]

            def load_pair(n):
                s = n % 2
                w_ok[n] = split_weights("wP", w_raw[:, :], w_hi[s][:, :], w_lo[s][:, :], wPair[n % NPAIR],
                                        free=[w_free[s], w_ok.get(n - 1)])

            def wp(n, a, z):
                return (w_hi[n % 2][:, a:z], w_lo[n % 2][:, a:z])

            xn_slots = [prob[0], prob[1]]
            free = {"xT": None, "lat": None}
            kv_free = [None] * NK
            q_free = [None, None]
            prob_free = [None] * NP_
            score_free = [None, None]
            out_free = [None, None]
            acc_free = {"accG": None, "accV": None, "oT": None, "part": None, "neg": None, "rden": None}
            q_ok, k_ok, v_ok, m_ok = {}, {}, {}, {}
            count = {"step": 0}
            load_pair(0)

            for b in range(NB):
                norm_free = None
                rstd_ok = layer_stats(range(b * NT, (b + 1) * NT), lambda k: X[:, k, :], lambda k: X_done[k])
                lat_ok = {}
                for j in range(NBLK):
                    s, k0 = j % 2, b * NT + j * TPB
                    xn = xn_slots[s][:, :, :].rearrange("p a (t c) -> p (a t) c", c=C)
                    need("vector", rstd_ok, prob_free[s])
                    ready = [normalise("vector", xn[:, t, :], X[:, k0 + t, :], k0 + t, "att_xn") for t in range(TPB)]
                    cols = slice(j * BLK, (j + 1) * BLK)
                    turned = transposed_tiles(k0, lambda t, xn=xn: xn[:, t, :], ready)
                    prob_free[s] = [turned[-1][2]]
                    for h, (n, ps, done) in enumerate(turned):
                        need("scalar", done, free["xT"])
                        hi = do("scalar", "att_xT_hi", lambda e, h=h, ps=ps, cols=cols: e.activation(xT_hi[:, h, cols], ps, ACT.Copy))
                        need("vector", hi, done)
                        lo = do("vector", "att_xT_lo", lambda e, h=h, ps=ps, cols=cols: e.tensor_tensor(xT_lo[:, h, cols], ps, xT_hi[:, h, cols], ALU.subtract))
                        bank_free[n] = [hi, lo]
                    n, ps = bank()
                    need("tensor", lo, kd_ok)
                    pairs = []
                    for c in range(CH):
                        pairs += terms((kd_hi[:, c, :], kd_lo[:, c, :]), (xT_hi[:, c, cols], xT_lo[:, c, cols]))
                    t = do("tensor", "latent", product(ps, pairs))
                    need("scalar", t, free["lat"])
                    hi = do("scalar", "lat_hi", lambda e, ps=ps, cols=cols: e.activation(lat_hi[:, cols], ps, ACT.Copy))
                    need("vector", hi, t)
                    lat_ok[j] = do("vector", "lat_lo", lambda e, ps=ps, cols=cols: e.tensor_tensor(lat_lo[:, cols], ps, lat_hi[:, cols], ALU.subtract))
                    bank_free[n] = [hi, lat_ok[j]]

                units = [(p, j) for p in range(NPAIR) for j in range(NBLK)]

                def slot_of(n, j):
                    return (n * NBLK + j) % NK

                def prepare(idx):
                    p, j = units[idx]
                    n = b * NPAIR + p
                    qs, ks = (n * NBLK + j) % 2, slot_of(n, j)
                    cols = slice(j * BLK, (j + 1) * BLK)
                    u_ = (n, j)
                    pieces = []

                    def query():
                        need("tensor", w_ok[n], lat_ok[j])
                        bn, ps = bank()
                        pairs = []
                        for c in range(CH):
                            pairs += terms(wp(n, c * P, (c + 1) * P), (xT_hi[:, c, cols], xT_lo[:, c, cols]))
                        done = do("tensor", "q_proj", product(ps, pairs))
                        free["xT"] = done
                        readers, dup = [], []
                        for h in range(2):
                            hi_, lo_ = slice(h * DH, (h + 1) * DH), slice((1 - h) * DH, (2 - h) * DH)
                            need("scalar", done, q_free[qs])
                            hi = do("scalar", "q_hi", lambda e, h=h, hi_=hi_: e.activation(
                                qA[qs][h][hi_, :], ps[hi_, :], ACT.Copy, scale=DH ** -0.5))
                            need("vector", hi, done, q_free[qs])
                            lo = do("vector", "q_lo", lambda e, h=h, hi_=hi_, lo_=lo_: e.scalar_tensor_tensor(
                                out=qA[qs][h][lo_, :], in0=ps[hi_, :], scalar=DH ** -0.5, in1=qA[qs][h][hi_, :],
                                op0=ALU.mult, op1=ALU.subtract))
                            need("sync", hi, q_free[qs])
                            dup.append(dma(f"qB_in{qs}{h}", qB[qs][h][0:DH, :].bitcast(F32), qA[qs][h][hi_, :].bitcast(F32)))
                            readers += [hi, lo]
                        bank_free[bn] = readers
                        q_ok[u_] = (readers, dup)

                    def key():
                        bn, ps = bank()
                        need("tensor", w_ok[n], lat_ok[j])
                        done = do("tensor", "k_proj", product(ps, terms(wp(n, 2 * P, 3 * P), (lat_hi[:, cols], lat_lo[:, cols]))))
                        readers, dup = [], []
                        for h in range(2):
                            hi_, lo_ = slice(h * DH, (h + 1) * DH), slice((1 - h) * DH, (2 - h) * DH)
                            need("scalar", done, kv_free[ks])
                            hi = do("scalar", "k_hi", lambda e, h=h, hi_=hi_: e.activation(kA[ks][h][hi_, :], ps[hi_, :], ACT.Copy))
                            need("vector", hi, done, kv_free[ks])
                            lo = do("vector", "k_lo", lambda e, h=h, hi_=hi_: e.tensor_tensor(
                                kB[ks][h][0:DH, :], ps[hi_, :], kA[ks][h][hi_, :], ALU.subtract))
                            need("sync", hi, kv_free[ks])
                            dup.append(dma(f"kA_in{ks}{h}", kA[ks][h][lo_, :].bitcast(F32), kA[ks][h][hi_, :].bitcast(F32)))
                            readers += [hi, lo]
                        bank_free[bn] = readers
                        k_ok[u_] = (readers, dup)

                    def value():
                        bn, ps = bank()
                        need("tensor", w_ok[n], lat_ok[j])
                        for t in range(TPB):
                            tc = slice(j * BLK + t * P, j * BLK + (t + 1) * P)
                            last = product(ps[:, t * P:(t + 1) * P], terms((lat_hi[:, tc], lat_lo[:, tc]), wp(n, 3 * P, 4 * P)))
                            if t < TPB - 1:
                                run("tensor", last)
                        done = do("tensor", "v_proj", last)
                        free["lat"] = done
                        need("scalar", done, kv_free[ks])
                        v_ok[u_] = do("scalar", "v_out", lambda e: e.activation(
                            V[ks][:, :, :], ps.rearrange("p (t d) -> p t d", d=P), ACT.Copy))
                        bank_free[bn] = [v_ok[u_]]

                    maxima = []

                    def maximum(h, t, c):
                        bn, ps = bank()
                        need("tensor", *q_ok[u_][0], *k_ok[n, c][0], *k_ok[n, c][1], ident_ok, const_ok)
                        width = BLK if c < j else (t + 1) * P
                        diag = c == j
                        last = product(ps[:, 0:width], [(qA[qs][h][:, t * P:(t + 1) * P], kA[slot_of(n, c)][h][:, 0:width])], last=not diag)
                        if diag:
                            run("tensor", last)
                            last = lambda e: e.matmul(ps[:, t * P:width], ident16[:, :], maskQ[:, :], start=False, stop=True)
                        done = do("tensor", "q_dot_k", last)
                        need("vector", done, acc_free["part"])
                        r = do("vector", "part_max", lambda e: e.reduce_max(part_max[:, h * TPB + t, c:c + 1], ps[:, 0:width], AX.X))
                        bank_free[bn] = [r]
                        maxima.append(r)

                    def minus_max():
                        need("vector", maxima[-1], acc_free["neg"])
                        t = do("vector", "row_max", lambda e: e.reduce_max(row_max[:, :], part_max[:, :, 0:j + 1], AX.X))
                        acc_free["part"] = t
                        need("vector", t)
                        t = do("vector", "neg_hi", lambda e: e.tensor_scalar(neg_r[:, :], row_max[:, :], -1.0, None, ALU.mult))
                        need("vector", t)
                        do("vector", "neg", lambda e: e.tensor_copy(
                            neg[:, :, :, 0], neg_r[:, :].bitcast(F32).rearrange("p (h t) -> p t h", h=2)))
                        t = do("vector", "neg", lambda e: e.scalar_tensor_tensor(
                            out=neg[:, :, :, 1], in0=row_max[:, :].rearrange("p (h t) -> p t h", h=2), scalar=-1.0,
                            in1=neg_r[:, :].bitcast(F32).rearrange("p (h t) -> p t h", h=2), op0=ALU.mult, op1=ALU.subtract))
                        bn, ps = bank()
                        need("tensor", t, ident_ok)
                        for tt in range(TPB):
                            f = lambda e, tt=tt: e.transpose(ps[0:4, tt * P:(tt + 1) * P],
                                                             neg[:, tt, :, :].rearrange("p a b -> p (a b)"), ident[:, :])
                            if tt < TPB - 1:
                                run("tensor", f)
                        done = do("tensor", "neg_turned", f)
                        acc_free["neg"] = done
                        need("scalar", done, q_free[qs])
                        for h in range(2):
                            m_ok[u_] = do("scalar", "neg_rows", lambda e, h=h: e.activation(qB[qs][h][DH:DH + 4, :], ps[0:4, :], ACT.Copy))
                        bank_free[bn] = [m_ok[u_]]

                    pieces = [key, query, value]
                    for c in range(j + 1):
                        for t in range(TPB):
                            for h in range(2):
                                pieces.append(lambda h=h, t=t, c=c: maximum(h, t, c))
                    pieces.append(minus_max)
                    if j == 1 and n + 1 < NB * NPAIR:
                        pieces.insert(3, lambda: load_pair(n + 1))
                    return pieces

                for f in prepare(0):
                    f()
                for idx, (p, j) in enumerate(units):
                    n = b * NPAIR + p
                    u_ = (n, j)
                    qs = (n * NBLK + j) % 2
                    os_ = (n * NBLK + j) % 2
                    nk = TPB * (j + 1)
                    ahead = prepare(idx + 1) if idx + 1 < len(units) else []
                    given = 0

                    def score(t):
                        st = count["step"] % 2
                        c, tt = divmod(t, TPB)
                        x0 = tt * P if c == j else 0
                        ks = slot_of(n, c)
                        need("tensor", score_free[st], *q_ok[u_][0], *q_ok[u_][1], m_ok[u_], *k_ok[n, c][0], *k_ok[n, c][1], sel_ok, const_ok)
                        for h in range(2):
                            kc = slice(tt * P, (tt + 1) * P)
                            run("tensor", product(scores[st][:, h, x0:], [(kA[ks][h][:, kc], qA[qs][h][:, x0:])], last=False))
                            if c == j:
                                run("tensor", lambda e, h=h: e.matmul(scores[st][:, h, x0:x0 + P], ident16[:, :], maskK[:, :], start=False, stop=False))
                            last = product(scores[st][:, h, x0:], [(kB[ks][h][:, kc], qB[qs][h][:, x0:])], first=False)
                            if h == 0:
                                run("tensor", last)
                        done = do("tensor", "score", last)
                        pr = count["step"] % NP_
                        need("scalar", done, prob_free[pr])
                        e_ok = do("scalar", "exp", lambda e: e.activation(prob[pr][:, :, x0:], scores[st][:, :, x0:], ACT.Exp))
                        score_free[st] = e_ok
                        count["step"] += 1
                        return pr, x0, e_ok

                    def weigh(t, pr, x0, e_ok):
                        c, tt = divmod(t, TPB)
                        need("tensor", e_ok, v_ok[n, c])
                        if t == 0:
                            need("tensor", out_free[os_])
                        for h in range(2):
                            f = lambda e, h=h: e.matmul(heads_out[os_][h * DH:(h + 1) * DH, x0:],
                                                        V[slot_of(n, c)][:, tt, h * DH:(h + 1) * DH], prob[pr][:, h, x0:],
                                                        start=(t == 0), stop=(t == nk - 1))
                            if h == 0:
                                run("tensor", f)
                        done = do("tensor", "weigh", f)
                        eng, acc, key_ = ("vector", accV, "accV") if t % 4 == 3 else ("gpsimd", accG, "accG")
                        need(eng, e_ok, acc_free[key_], state.get(key_))
                        if state.get(key_) is None:
                            if x0:
                                z0 = do(eng, f"{key_}_zero", lambda e: e.memset(acc[:, :, 0:x0], 0.0))
                            a = do(eng, key_, lambda e: e.tensor_copy(acc[:, :, x0:], prob[pr][:, :, x0:]))
                            if x0:
                                a = [z0, a]
                        else:
                            a = do(eng, key_, lambda e: e.tensor_tensor(acc[:, :, x0:], acc[:, :, x0:], prob[pr][:, :, x0:], ALU.add))
                        state[key_] = a
                        prob_free[pr] = [done, a]
                        return done

                    state = {}
                    prev = None
                    for t in range(nk):
                        cur = (t,) + score(t)
                        want = len(ahead) * (t + 1) // nk
                        half = (given + want) // 2
                        while given < half:
                            ahead[given]()
                            given += 1
                        if prev is not None:
                            weigh(*prev)
                        while given < want:
                            ahead[given]()
                            given += 1
                        prev = cur
                    done = weigh(*prev)
                    q_free[qs] = done
                    if j == NBLK - 1:
                        for c in range(NBLK):
                            kv_free[slot_of(n, c)] = done
                    need("gpsimd", state["accG"], state["accV"])
                    t = do("gpsimd", "acc_sum", lambda e: e.tensor_tensor(accG[:, :, :], accG[:, :, :], accV[:, :, :], ALU.add))
                    acc_free["accV"] = t
                    bn, ps = bank()
                    need("tensor", t, ones_ok)
                    run("tensor", lambda e, ps=ps: e.matmul(ps[0:DH, :], ones[:, :], accG[:, 0, :], start=True, stop=True))
                    t = do("tensor", "denominator", lambda e, ps=ps: e.matmul(ps[DH:P, :], ones[:, :], accG[:, 1, :], start=True, stop=True))
                    acc_free["accG"] = t
                    need("vector", t, acc_free["rden"])
                    r = do("vector", "rden", lambda e, ps=ps: e.reciprocal(rden[:, :], ps))
                    bank_free[bn] = [r]
                    need("vector", r, done, acc_free["oT"])
                    o = do("vector", "oT", lambda e, os_=os_: e.tensor_tensor(oT[:, :], heads_out[os_][:, :], rden[:, :], ALU.mult))
                    out_free[os_] = o
                    acc_free["rden"] = o
                    need("scalar", o, acc_free["oT"])
                    hi = do("scalar", "oT_hi", lambda e: e.activation(oT_hi[:, :], oT[:, :], ACT.Copy))
                    need("gpsimd", hi, o)
                    lo = do("gpsimd", "oT_lo", lambda e: e.tensor_tensor(oT_lo[:, :], oT[:, :], oT_hi[:, :], ALU.subtract))
                    need("tensor", lo)
                    for t0 in range(0, TPB, 2):
                        bn, ps = bank()
                        for q in range(2):
                            cs = slice((t0 + q) * P, (t0 + q + 1) * P)
                            y = do("tensor", "att_y", product(ps[:, q * C:(q + 1) * C],
                                   terms((oT_hi[:, cs], oT_lo[:, cs]), wp(n, 4 * P, 4 * P + C))))
                        k = b * NT + j * TPB + t0
                        need("vector", y, X_done[k])
                        X_done[k] = X_done[k + 1] = [do("vector", "x_plus_att", lambda e, k=k, ps=ps: e.tensor_tensor(
                            X[:, k:k + 2, :], X[:, k:k + 2, :], ps.rearrange("p (t c) -> p t c", c=C), ALU.add))]
                        bank_free[bn] = X_done[k]
                    acc_free["oT"] = [y, lo]
                    w_free[n % 2] = y

        for i in range(2, 8):
            bank_free[i] = pg.everything_so_far()
        channel_mixer("b", True)


def kernel(L0_attn_a_u, L0_attn_a_A_diag, L0_attn_a_Bmat, L0_attn_a_Cmat, L0_attn_a_Dmat, L0_attn_a_h0,
           L0_attn_a_ln_gamma, L0_attn_a_ln_beta, L0_attn_b_w_kv_down, L0_attn_b_w_kv_up, L0_attn_b_w_q,
           L0_attn_b_w_out, L0_ffn_W_r, L0_ffn_W_k, L0_ffn_W_v, L0_ffn_mu_r, L0_ffn_mu_k):
    import numpy as np
    import concourse.bacc as bacc
    from concourse.bass_utils import run_bass_kernel_spmd

    def halves(w):
        return np.asarray(w).reshape(CH, P, -1).transpose(1, 0, 2)

    def cols(v):
        return np.asarray(v).reshape(CH, P).T

    wq, up, wo = np.asarray(L0_attn_b_w_q), np.asarray(L0_attn_b_w_kv_up), np.asarray(L0_attn_b_w_out)
    HD = NH * DH
    pair = [np.concatenate([halves(wq[:, i:i + P]).reshape(P, CH * P), up[:, i:i + P], up[:, HD + i:HD + i + P],
                            wo[i:i + P, :]], axis=1) for i in range(0, HD, P)]
    arrays = {
        "u": np.asarray(L0_attn_a_u).reshape(NB * T, C),
        "wA": np.stack([halves(np.asarray(w).T) for w in (L0_attn_a_Bmat, L0_attn_a_Cmat, L0_attn_a_Dmat)], axis=1),
        "wF": np.stack([halves(np.asarray(w).T) for w in (L0_ffn_W_r, L0_ffn_W_k, L0_ffn_W_v)], axis=1),
        "wKD": halves(L0_attn_b_w_kv_down),
        "wPair": np.stack(pair),
        "aDiag": cols(L0_attn_a_A_diag),
        "h0": cols(L0_attn_a_h0),
        "gb": np.broadcast_to(np.stack([np.asarray(L0_attn_a_ln_gamma), np.asarray(L0_attn_a_ln_beta)])[None], (P, 2, C)),
        "mu": np.stack([cols(L0_ffn_mu_r), cols(L0_ffn_mu_k)], axis=1),
    }
    arrays = {k: np.ascontiguousarray(v) for k, v in arrays.items()}
    nc = bacc.Bacc("TRN2", target_bir_lowering=False, num_devices=1)
    args = [nc.dram_tensor(k, v.shape, mybir.dt.from_np(v.dtype), kind="ExternalInput").ap() for k, v in arrays.items()]
    out = nc.dram_tensor("out", (NB * T, C), F32, kind="ExternalOutput").ap()
    build(nc, *args, out)
    r = run_bass_kernel_spmd(nc, [arrays], core_ids=[0])
    return r.results[0]["out"].reshape(NB, T, C)
```

```python
from contextlib import ExitStack

import concourse.bass as bass
from concourse import mybir

ALU = mybir.AluOpType
ACT = mybir.ActivationFunctionType
AX = mybir.AxisListType
F32 = mybir.dt.float32
F32R = mybir.dt.float32r
BF16 = mybir.dt.bfloat16

P = 128
NB, T, C = 2, 2048, 256
CH = C // P
BLK = 512
NBLK = T // BLK
TPB = BLK // P
NT = T // P
NH, DH = 16, 64
NPAIR = NH // 2
RANK = 128
EPS = 1e-5
CLAMP = 1e6
MASKED = -3.0e38
WPC = 2 * P + P + P + C
VSHARE = (99, 99, 4, 3)
NSCORE = 3
QUAD = 32
DSUB = 2
DCH = 2 * BLK // (4 * DSUB)
NPROB = 4
NK = NBLK + 1


class Program:

    def __init__(self, nc, ctx):
        self.nc, self.ctx = nc, ctx
        self.engine = {"tensor": nc.tensor, "vector": nc.vector, "scalar": nc.scalar,
                       "gpsimd": nc.gpsimd, "sync": nc.sync}
        self.sems, self.value, self.waited = {}, {}, {}

    def do(self, engine, step, make):
        return self._signal(engine, step, make, 1)

    def dma(self, step, out, in_):
        return self._signal("sync", step, lambda e: e.dma_start(out, in_), 16)

    def _signal(self, engine, step, make, by):
        if step not in self.sems:
            self.sems[step] = self.ctx.enter_context(self.nc.semaphore(step))
            self.value[step] = 0
        self.value[step] += by
        sem = self.sems[step]
        make(self.engine[engine]).then_inc(sem, by)
        return step, self.value[step]

    def run(self, engine, make):
        make(self.engine[engine])

    def need(self, engine, *done):
        for d in done:
            if d is None:
                continue
            if isinstance(d, list):
                self.need(engine, *d)
                continue
            step, value = d
            if self.waited.get((engine, step), 0) < value:
                self.waited[engine, step] = value
                self.engine[engine].wait_ge(self.sems[step], value)

    def everything_so_far(self):
        return [(s, v) for s, v in self.value.items()]


def build(nc, u, wA, wF, wKD, wPair, aDiag, h0, gb, mu, out):
    ctx = ExitStack()
    with ctx:
        pg = Program(nc, ctx)
        do, dma, run, need = pg.do, pg.dma, pg.run, pg.need

        def sb(where, name, shape, dt=F32):
            return where.enter_context(nc.sbuf_tensor(name, shape, dt))

        scores = ctx.enter_context(nc.psum_tensor("scores", [P, NSCORE, BLK], F32))
        heads_out = ctx.enter_context(nc.psum_tensor("heads_out", [P, BLK], F32))
        work = [ctx.enter_context(nc.psum_tensor(f"work{i}", [P, 2, BLK], F32)) for i in range(2)]
        banks = ([scores[:, i, :] for i in range(NSCORE)] + [heads_out[:, :]]
                 + [w[:, i, :] for w in work for i in range(2)])
        bank_free = {}
        turn = {"next": 0}

        def bank():
            n = turn["next"] % len(banks)
            turn["next"] += 1
            need("tensor", bank_free.get(n))
            return n, banks[n]

        def bank_pair():
            n = turn["next"] % len(work)
            turn["next"] += 1
            need("tensor", bank_free.get(n))
            return n, work[n]

        X = sb(ctx, "X", [P, NB * NT, C])
        ident = sb(ctx, "ident", [P, P])
        ident16 = sb(ctx, "ident16", [P, P], BF16)
        mean_var = sb(ctx, "mean_var", [P, NB * NT, 2])
        stats = sb(ctx, "stats", [P, 4, 6])
        std = sb(ctx, "std", [P, NB * NT])
        rstd = sb(ctx, "rstd", [P, NB * NT])

        x_in = []
        for b in range(NB):
            for j in range(NBLK):
                k = (b * NBLK + j)
                x_in.append(dma(f"x_in{k}", X[:, k * TPB:(k + 1) * TPB, :],
                                u[k * BLK:(k + 1) * BLK, :].rearrange("(t p) c -> p t c", p=P)))
        X_done = {k: [x_in[k // TPB]] for k in range(NB * NT)}

        z = [do("gpsimd", "ident_zero", lambda e: e.memset(ident[:, :], 0.0)),
             do("gpsimd", "ident_zero", lambda e: e.memset(ident16[:, :], 0.0))]
        need("gpsimd", z)
        for m in (ident, ident16):
            ident_ok = do("gpsimd", "ident", lambda e, m=m: e.affine_select(
                out=m[:, :], in_=m[:, :], compare_op=ALU.not_equal, fill=1.0, base=0,
                pattern=[[-1, P]], channel_multiplier=1))

        stats_free = [None] * 4
        norm_free = {"last": None}

        def tile_stats(k, src, ready):
            slot = k % 4
            need("vector", ready, stats_free[slot], norm_free["last"])
            need("vector", do("vector", "bn_stats", lambda e: e.bn_stats(stats[:, slot, :], src)))
            stats_free[slot] = do("vector", "bn_aggr", lambda e: e.bn_aggr(mean_var[:, k, :], stats[:, slot, :]))

        def inverse_std(a, z):
            need("vector", *stats_free)
            t = do("vector", "var_eps", lambda e: e.tensor_scalar(std[:, a:z], mean_var[:, a:z, 1], EPS, None, ALU.add))
            need("scalar", t)
            t = do("scalar", "std", lambda e: e.activation(std[:, a:z], std[:, a:z], ACT.Sqrt))
            need("vector", t)
            return do("vector", "rstd", lambda e: e.reciprocal(rstd[:, a:z], std[:, a:z]))

        def normalise(dst, src, k, step):
            norm_free["last"] = do("vector", step, lambda e: e.tensor_scalar(
                dst, src, mean_var[:, k, 0:1], rstd[:, k:k + 1], ALU.subtract, ALU.mult))
            return norm_free["last"]

        def terms(a, b):
            return [(a[0], b[0]), (a[0], b[1]), (a[1], b[0])]

        def product(dst, pairs, first=True, last=True):
            made = []
            for n, (l, r) in enumerate(pairs):
                made.append(lambda e, l=l, r=r, s=(first and n == 0), z=(last and n == len(pairs) - 1):
                            e.matmul(dst, l, r, start=s, stop=z))
            for m in made[:-1]:
                run("tensor", m)
            return made[-1]

        def split_weights(name, raw, hi, lo, src, free=None):
            need("sync", free)
            t = dma(f"{name}_in", raw, src)
            need("vector", t, free)
            t = do("vector", f"{name}_hi", lambda e: e.tensor_copy(hi, raw))
            need("vector", t)
            return do("vector", f"{name}_lo", lambda e: e.tensor_tensor(lo, raw, hi, ALU.subtract))

        def transposed_tiles(k0, xn_of, ready):
            res = []
            for h in range(CH):
                n, ps = bank()
                for t in range(TPB):
                    need("tensor", ready[t], ident_ok)
                    f = lambda e, t=t, h=h, ps=ps: e.transpose(
                        ps[:, t * P:(t + 1) * P], xn_of(t)[:, h * P:(h + 1) * P], ident[:, :])
                    if t < TPB - 1:
                        run("tensor", f)
                done = do("tensor", "x_turned", f)
                res.append((n, ps, done))
            return res

        tail_scope = ctx.enter_context(ExitStack())
        gamma_beta = sb(tail_scope, "gamma_beta", [P, 2, C])
        G = sb(tail_scope, "G", [P, NB * NT, C])
        nrm = sb(tail_scope, "nrm", [P, 2, 2, C])
        clp = sb(tail_scope, "clp", [P, 2, 2, C])
        msk = sb(tail_scope, "msk", [P, 2, 2, C])
        fin = sb(tail_scope, "fin", [P, 2, 2, C], mybir.dt.uint32)
        G_done, act_rstd, beta_ok = {}, {}, {}
        nrm_free, tail_free = [None, None], [None, None]

        def tail_norm(k):
            s = (k // 2) % 2
            need("vector", act_rstd[k // NT], nrm_free[s])
            for q in range(2):
                t = normalise(nrm[:, s, q, :], G[:, k + q, :], k + q, "act_norm")
            need("gpsimd", t, small_in)
            both = [gamma_beta[:, i:i + 1, :].broadcast_to([P, 2, C]) for i in range(2)]
            t = do("gpsimd", "act_gamma", lambda e: e.tensor_tensor(nrm[:, s, :, :], nrm[:, s, :, :], both[0], ALU.mult))
            need("gpsimd", t)
            beta_ok[k] = do("gpsimd", "act_beta", lambda e: e.tensor_tensor(nrm[:, s, :, :], nrm[:, s, :, :], both[1], ALU.add))

        def tail_add(k):
            s = (k // 2) % 2
            need("vector", beta_ok[k], tail_free[s])
            t = do("vector", "clamp", lambda e: e.tensor_scalar(clp[:, s, :, :], nrm[:, s, :, :], -CLAMP, CLAMP, ALU.max, ALU.min))
            m = do("vector", "not_nan", lambda e: e.tensor_tensor(msk[:, s, :, :], nrm[:, s, :, :], nrm[:, s, :, :], ALU.is_equal))
            f = do("vector", "is_finite", lambda e: e.tensor_scalar(fin[:, s, :, :], nrm[:, s, :, :], 0.0, 0.0, ALU.mult, ALU.is_equal))
            need("vector", t, m)
            t = do("vector", "no_nan", lambda e: e.tensor_tensor(clp[:, s, :, :], clp[:, s, :, :], msk[:, s, :, :], ALU.mult))
            need("vector", t, f)
            t = do("vector", "nan_to_num", lambda e: e.copy_predicated(clp[:, s, :, :], fin[:, s, :, :], nrm[:, s, :, :]))
            nrm_free[s] = t
            need("gpsimd", t)
            X_done[k] = X_done[k + 1] = [do("gpsimd", "x_plus_ssm", lambda e: e.tensor_tensor(
                X[:, k:k + 2, :], X[:, k:k + 2, :], clp[:, s, :, :], ALU.add))]
            tail_free[s] = X_done[k]

        def tail_pieces(b):
            ks = list(range(b * NT, (b + 1) * NT, 2))
            pieces = []
            for n, k in enumerate(ks):
                pieces.append(lambda k=k: tail_norm(k))
                if n:
                    pieces.append(lambda k=k: tail_add(k - 2))
            return pieces + [lambda: tail_add(ks[-1])]

        def spread(pieces, n):
            return [pieces[len(pieces) * i // n:len(pieces) * (i + 1) // n] for i in range(n)]

        with ExitStack() as ph:
            w_raw = sb(ph, "wA_raw", [P, 3, CH, C])
            w_hi = sb(ph, "wA_hi", [P, 3, CH, C], F32R)
            w_lo = sb(ph, "wA_lo", [P, 3, CH, C], F32R)
            a_in = sb(ph, "a_in", [P, CH])
            a_abs = sb(ph, "a_abs", [P, CH])
            a_log = sb(ph, "a_log", [P, CH])
            a_col = sb(ph, "a_col", [P, CH])
            zeros = sb(ph, "zeros", [P, BLK])
            decay = sb(ph, "decay", [P, CH, BLK])
            state0 = sb(ph, "state0", [P, CH])
            xn = sb(ph, "xn", [P, 2, TPB, C])
            xT_hi = sb(ph, "xT_hi", [P, 3, CH, BLK], F32R)
            xT_lo = sb(ph, "xT_lo", [P, 3, CH, BLK], F32R)
            xs = sb(ph, "xs", [P, 2, CH, BLK])
            xs_hi = sb(ph, "xs_hi", [P, 2, CH, BLK], F32R)
            xs_lo = sb(ph, "xs_lo", [P, 2, CH, BLK], F32R)
            small_in = dma("ssm_small_in", a_in[:, :], aDiag)
            small_in = dma("ssm_small_in", state0[:, :], h0)
            small_in = dma("ssm_small_in", gamma_beta[:, :, :], gb)
            wA_ok = split_weights("wA", w_raw[:, :, :, :], w_hi[:, :, :, :], w_lo[:, :, :, :], wA)
            zeros_ok = do("vector", "zeros", lambda e: e.memset(zeros[:, :], 0.0))
            need("vector", small_in)
            t = do("vector", "softplus_v", lambda e: e.tensor_scalar(a_abs[:, :], a_in[:, :], -1.0, None, ALU.mult))
            need("vector", t)
            t = do("vector", "softplus_v", lambda e: e.tensor_tensor(a_abs[:, :], a_abs[:, :], a_in[:, :], ALU.min))
            need("scalar", t)
            t = do("scalar", "softplus_a", lambda e: e.activation(a_log[:, :], a_abs[:, :], ACT.Exp))
            need("scalar", t)
            t = do("scalar", "softplus_a", lambda e: e.activation(a_log[:, :], a_log[:, :], ACT.Ln, bias=1.0))
            need("vector", t)
            t = do("vector", "softplus_v", lambda e: e.scalar_tensor_tensor(
                out=a_col[:, :], in0=a_in[:, :], scalar=0.0, in1=a_log[:, :], op0=ALU.max, op1=ALU.add))
            need("vector", t, zeros_ok)
            for h in range(CH):
                decay_ok = do("vector", "decay", lambda e, h=h: e.tensor_scalar(
                    decay[:, h, :], zeros[:, :], a_col[:, h:h + 1], None, ALU.subtract))

            xn_free, xT_free, xs_free = [None, None], [None] * 3, [None, None]
            scanned, turned_ok, ssm_rstd = {}, {}, {}

            def x_stats(b):
                for k in range(b * NT, (b + 1) * NT):
                    tile_stats(k, X[:, k, :], X_done[k])
                ssm_rstd[b] = inverse_std(b * NT, (b + 1) * NT)

            def ssm_front(i):
                s, x, k0 = i % 2, i % 3, i * TPB
                need("vector", ssm_rstd[i // NBLK], xn_free[s])
                ready = [normalise(xn[:, s, t, :], X[:, k0 + t, :], k0 + t, "ssm_xn") for t in range(TPB)]
                turned = transposed_tiles(k0, lambda t: xn[:, s, t, :], ready)
                xn_free[s] = turned[-1][2]
                for h, (n, ps, done) in enumerate(turned):
                    need("scalar", done, xT_free[x])
                    hi = do("scalar", "ssm_xT_hi", lambda e: e.activation(xT_hi[:, x, h, :], ps, ACT.Copy))
                    need("vector", hi, done)
                    turned_ok[i] = do("vector", "ssm_xT_lo", lambda e: e.tensor_tensor(
                        xT_lo[:, x, h, :], ps, xT_hi[:, x, h, :], ALU.subtract))
                    bank_free[n] = [hi, turned_ok[i]]

            def ssm_states(i):
                s, x = i % 2, i % 3
                b, j = divmod(i, NBLK)
                need("tensor", turned_ok[i], wA_ok)
                for m in range(CH):
                    n, ps = bank()
                    pairs = []
                    for c in range(CH):
                        pairs += terms((w_hi[:, 0, c, m * P:(m + 1) * P], w_lo[:, 0, c, m * P:(m + 1) * P]),
                                       (xT_hi[:, x, c, :], xT_lo[:, x, c, :]))
                    bu = do("tensor", "bu", product(ps, pairs))
                    need("vector", bu, decay_ok, small_in, scanned.get((b, j - 1, m)), xs_free[s])
                    init = state0[:, m:m + 1] if j == 0 else xs[:, 1 - s, m, BLK - 1:BLK]
                    sc = do("vector", "scan", lambda e: e.tensor_tensor_scan(
                        xs[:, s, m, :], decay[:, m, :], ps, init, ALU.mult, ALU.add))
                    scanned[b, j, m] = sc
                    bank_free[n] = [sc]
                    need("scalar", sc, xs_free[s])
                    hi = do("scalar", "xs_hi", lambda e: e.activation(xs_hi[:, s, m, :], xs[:, s, m, :], ACT.Copy))
                    need("gpsimd", hi, sc, xs_free[s])
                    scanned[i, "parts"] = do("gpsimd", "xs_lo", lambda e: e.tensor_tensor(
                        xs_lo[:, s, m, :], xs[:, s, m, :], xs_hi[:, s, m, :], ALU.subtract))

            def ssm_output(i):
                s, x = i % 2, i % 3
                need("tensor", scanned[i, "parts"])
                for t in range(0, TPB, 2):
                    n, ps = bank()
                    for q in range(2):
                        cols = slice((t + q) * P, (t + q + 1) * P)
                        pairs = []
                        for c in range(CH):
                            pairs += terms((xT_hi[:, x, c, cols], xT_lo[:, x, c, cols]),
                                           (w_hi[:, 2, c, :], w_lo[:, 2, c, :]))
                        for c in range(CH):
                            pairs += terms((xs_hi[:, s, c, cols], xs_lo[:, s, c, cols]),
                                           (w_hi[:, 1, c, :], w_lo[:, 1, c, :]))
                        y = do("tensor", "ssm_y", product(ps[:, q * C:(q + 1) * C], pairs))
                    kk = i * TPB + t
                    need("scalar", y)
                    g = do("scalar", "gelu", lambda e: e.activation(
                        G[:, kk:kk + 2, :], ps.rearrange("p (t c) -> p t c", c=C), ACT.Gelu))
                    bank_free[n] = [g]
                    G_done[kk] = G_done[kk + 1] = g
                xT_free[x] = y
                xs_free[s] = [y, scanned[i, "parts"]]

            def ssm_stats(i):
                for k in range(i * TPB, (i + 1) * TPB):
                    tile_stats(k, G[:, k, :], G_done[k])

            nb = NB * NBLK
            x_stats(0)
            ssm_front(0)
            ssm_front(1)
            ssm_states(0)
            tail = spread(tail_pieces(0), NBLK - 1)
            for i in range(nb):
                if i == 0:
                    x_stats(1)
                if i + 2 < nb:
                    ssm_front(i + 2)
                if i + 1 < nb:
                    ssm_states(i + 1)
                ssm_output(i)
                if i % NBLK:
                    ssm_stats(i - 1)
                if i % NBLK == NBLK - 1:
                    ssm_stats(i)
                    act_rstd[i // NBLK] = inverse_std((i + 1 - NBLK) * TPB, (i + 1) * TPB)
                elif i >= NBLK:
                    for f in tail[i - NBLK]:
                        f()
            ssm_memory = pg.everything_so_far()

        def channel_mixer(tag, store, before, between=()):
            with ExitStack() as ph:
                w_raw = sb(ph, f"wF_raw{tag}", [P, 3, CH, C])
                w_hi = sb(ph, f"wF_hi{tag}", [P, 3, CH, C], F32R)
                w_lo = sb(ph, f"wF_lo{tag}", [P, 3, CH, C], F32R)
                mu_sb = sb(ph, f"mu{tag}", [P, 2, CH])
                one_mu = sb(ph, f"one_mu{tag}", [P, 2, CH])
                xn = sb(ph, f"xnF{tag}", [P, 2, TPB, C])
                xT = sb(ph, f"xTF{tag}", [P, 2, CH, BLK + 1])
                old = sb(ph, f"old{tag}", [P, CH, BLK])
                mix = sb(ph, f"mix{tag}", [P, CH, BLK])
                mix_hi = sb(ph, f"mix_hi{tag}", [P, 2, 2, CH, BLK], F32R)
                mix_lo = sb(ph, f"mix_lo{tag}", [P, 2, 2, CH, BLK], F32R)
                relu = sb(ph, f"relu{tag}", [P, CH, BLK])
                kact = sb(ph, f"kact{tag}", [P, CH, BLK])
                kact_hi = sb(ph, f"kact_hi{tag}", [P, 2, CH, BLK], F32R)
                kact_lo = sb(ph, f"kact_lo{tag}", [P, 2, CH, BLK], F32R)
                gate = sb(ph, f"gate{tag}", [P, 2, TPB, C])
                upd = sb(ph, f"upd{tag}", [P, 2, TPB, C])
                for e in ("sync", "tensor", "vector", "scalar", "gpsimd"):
                    need(e, before)
                mu_in = dma("mu_in", mu_sb[:, :, :], mu)
                w_ok = split_weights("wF", w_raw[:, :, :, :], w_hi[:, :, :, :], w_lo[:, :, :, :], wF)
                need("vector", mu_in)
                mu_ok = do("vector", "one_minus_mu", lambda e: e.tensor_scalar(one_mu[:, :, :], mu_sb[:, :, :], -1.0, 1.0, ALU.mult, ALU.add))
                xn_free, xT_free, mix_free, kact_free, gate_free, relu_free = ([None, None] for _ in range(6))
                mixf = [None, None]
                stored = []
                rstd_ok, k_parts, relu_ok, gate_ok, k_read = {}, {}, {}, {}, {}

                def ffn_stats(b):
                    for k in range(b * NT, (b + 1) * NT):
                        tile_stats(k, X[:, k, :], X_done[k])
                    rstd_ok[b] = inverse_std(b * NT, (b + 1) * NT)

                def front(i):
                    b, j = divmod(i, NBLK)
                    s, k0 = i % 2, i * TPB
                    need("vector", rstd_ok[b], xn_free[s])
                    ready = [normalise(xn[:, s, t, :], X[:, k0 + t, :], k0 + t, "ffn_xn") for t in range(TPB)]
                    turned = transposed_tiles(k0, lambda t: xn[:, s, t, :], ready)
                    xn_free[s] = turned[-1][2]
                    if j == 0:
                        need("vector", xT_free[s])
                        edge = do("vector", "ffn_edge", lambda e: e.memset(xT[:, s, :, 0:1], 0.0))
                    else:
                        need("vector", xT_free[s], xT_state["ok"])
                        edge = do("vector", "ffn_edge", lambda e: e.tensor_copy(xT[:, s, :, 0:1], xT[:, 1 - s, :, BLK:BLK + 1]))
                    oks = []
                    for h, (n, ps, done) in enumerate(turned):
                        need("scalar", done, xT_free[s])
                        t = do("scalar", "ffn_xT", lambda e, h=h, ps=ps: e.activation(xT[:, s, h, 1:BLK + 1], ps, ACT.Copy))
                        bank_free[n] = [t]
                        oks.append(t)
                    xT_state["ok"] = oks[-1]
                    for r in range(2):
                        for h in range(CH):
                            need("vector", oks[h], edge, mu_ok, mixf[h])
                            t = do("vector", "mix_old", lambda e, r=r, h=h: e.tensor_scalar(
                                old[:, h, :], xT[:, s, h, 0:BLK], one_mu[:, r, h:h + 1], None, ALU.mult))
                            need("vector", t)
                            t = do("vector", "mix", lambda e, r=r, h=h: e.scalar_tensor_tensor(
                                out=mix[:, h, :], in0=xT[:, s, h, 1:BLK + 1], scalar=mu_sb[:, r, h:h + 1],
                                in1=old[:, h, :], op0=ALU.mult, op1=ALU.add))
                            xT_free[s] = t
                            need("scalar", t, mix_free[s])
                            hi = do("scalar", "mix_hi", lambda e, r=r, h=h: e.activation(mix_hi[:, s, r, h, :], mix[:, h, :], ACT.Copy))
                            need("gpsimd", hi, t, mix_free[s])
                            lo = do("gpsimd", "mix_lo", lambda e, r=r, h=h: e.tensor_tensor(
                                mix_lo[:, s, r, h, :], mix[:, h, :], mix_hi[:, s, r, h, :], ALU.subtract))
                            mixf[h] = lo
                    mixed[i] = lo

                xT_state, mixed = {"ok": None}, {}

                def products(i):
                    s = i % 2
                    need("tensor", mixed[i], w_ok)
                    for m in range(CH):
                        n, ps = bank()
                        pairs = []
                        for c in range(CH):
                            pairs += terms((w_hi[:, 1, c, m * P:(m + 1) * P], w_lo[:, 1, c, m * P:(m + 1) * P]),
                                           (mix_hi[:, s, 1, c, :], mix_lo[:, s, 1, c, :]))
                        t = do("tensor", "ffn_k", product(ps, pairs))
                        need("scalar", t, relu_free[m])
                        relu_ok[m] = do("scalar", "ffn_relu", lambda e: e.activation(relu[:, m, :], ps, ACT.Relu))
                        bank_free[n] = [relu_ok[m]]
                    for t0 in range(0, TPB, 2):
                        n, ps = bank()
                        for q in range(2):
                            cols = slice((t0 + q) * P, (t0 + q + 1) * P)
                            pairs = []
                            for c in range(CH):
                                pairs += terms((mix_hi[:, s, 0, c, cols], mix_lo[:, s, 0, c, cols]),
                                               (w_hi[:, 0, c, :], w_lo[:, 0, c, :]))
                            t = do("tensor", "ffn_r", product(ps[:, q * C:(q + 1) * C], pairs))
                        need("scalar", t, gate_free[s])
                        gate_ok[i] = do("scalar", "sigmoid", lambda e: e.activation(
                            gate[:, s, t0:t0 + 2, :], ps.rearrange("p (t c) -> p t c", c=C), ACT.Sigmoid))
                        bank_free[n] = [gate_ok[i]]
                    mix_free[s] = t

                def square(i):
                    s = i % 2
                    for m in range(CH):
                        need("vector", relu_ok[m], relu_free[m])
                        t = do("vector", "ffn_square", lambda e: e.tensor_tensor(kact[:, m, :], relu[:, m, :], relu[:, m, :], ALU.mult))
                        need("vector", t, kact_free[s])
                        hi = do("vector", "kact_hi", lambda e: e.tensor_copy(kact_hi[:, s, m, :], kact[:, m, :]))
                        need("vector", hi)
                        k_parts[i] = relu_free[m] = do("vector", "kact_lo", lambda e: e.tensor_tensor(
                            kact_lo[:, s, m, :], kact[:, m, :], kact_hi[:, s, m, :], ALU.subtract))

                def update(i):
                    s, k0 = i % 2, i * TPB
                    need("tensor", k_parts[i], w_ok)
                    for t0 in range(0, TPB, 2):
                        n, ps = bank()
                        for q in range(2):
                            cols = slice((t0 + q) * P, (t0 + q + 1) * P)
                            pairs = []
                            for c in range(CH):
                                pairs += terms((kact_hi[:, s, c, cols], kact_lo[:, s, c, cols]),
                                               (w_hi[:, 2, c, :], w_lo[:, 2, c, :]))
                            t = do("tensor", "ffn_v", product(ps[:, q * C:(q + 1) * C], pairs))
                        need("vector", t, gate_ok[i], gate_free[s])
                        t2 = do("vector", "gated", lambda e: e.tensor_tensor(
                            upd[:, s, t0:t0 + 2, :], ps.rearrange("p (t c) -> p t c", c=C), gate[:, s, t0:t0 + 2, :], ALU.mult))
                        bank_free[n] = [t2]
                        need("gpsimd", t2)
                        k = k0 + t0
                        X_done[k] = X_done[k + 1] = [do("gpsimd", "x_plus_ffn", lambda e: e.tensor_tensor(
                            X[:, k:k + 2, :], X[:, k:k + 2, :], upd[:, s, t0:t0 + 2, :], ALU.add))]
                    kact_free[s] = t
                    gate_free[s] = X_done[k]
                    if store:
                        need("sync", X_done[k0], X_done[k0 + TPB - 1])
                        stored.append(dma("stored", out[i * BLK:(i + 1) * BLK, :].rearrange("(t p) c -> p t c", p=P),
                                          X[:, k0:k0 + TPB, :]))

                nb = NB * NBLK
                between = spread(list(between), NBLK - 1) + [[]] * (nb + 1)
                ffn_stats(0)
                front(0)
                for i in range(nb + 1):
                    if i < nb:
                        products(i)
                    for f in between[i]:
                        f()
                    if i == NBLK - 1:
                        ffn_stats(1)
                    if i + 1 < nb:
                        front(i + 1)
                    if i < nb:
                        square(i)
                    if i:
                        update(i - 1)
                if store:
                    need("sync", stored[-1])

        channel_mixer("a", False, ssm_memory, tail_pieces(1))
        tail_scope.close()

        before = pg.everything_so_far()
        with ExitStack() as ph:
            xT_hi = sb(ph, "att_xT_hi", [P, CH, T], F32R)
            xT_lo = sb(ph, "att_xT_lo", [P, CH, T], F32R)
            lat_hi = sb(ph, "lat_hi", [P, T], F32R)
            lat_lo = sb(ph, "lat_lo", [P, T], F32R)
            kd_hi = sb(ph, "kd_hi", [P, CH, RANK], F32R)
            kd_lo = sb(ph, "kd_lo", [P, CH, RANK], F32R)
            w_raw = sb(ph, "wP_raw", [P, WPC])
            w_hi = [sb(ph, f"wP_hi{i}", [P, WPC], F32R) for i in range(2)]
            w_lo = [sb(ph, f"wP_lo{i}", [P, WPC], F32R) for i in range(2)]
            qA = [[sb(ph, f"qA{i}{h}", [P, BLK], F32R) for h in range(2)] for i in range(2)]
            qB = [[sb(ph, f"qB{i}{h}", [DH + 4, BLK], F32R) for h in range(2)] for i in range(2)]
            kA = [[sb(ph, f"kA{i}{h}", [P, BLK], F32R) for h in range(2)] for i in range(NK)]
            kB = [[sb(ph, f"kB{i}{h}", [DH + 4, BLK], F32R) for h in range(2)] for i in range(NK)]
            V = [sb(ph, f"V{i}", [P, TPB, P]) for i in range(NK)]
            prob = [sb(ph, f"prob{i}", [P, 2, BLK]) for i in range(NPROB)]
            xn = [sb(ph, f"att_xn{i}", [P, C]) for i in range(2)]
            accG = [sb(ph, f"accG{i}", [P, 2, BLK]) for i in range(2)]
            accV = [sb(ph, f"accV{i}", [P, 2, BLK]) for i in range(2)]
            pick = sb(ph, "pick", [P, DSUB, QUAD // DSUB, DSUB])
            sel = accG[0]
            maskQ = sb(ph, "maskQ", [P, P], BF16)
            maskK = sb(ph, "maskK", [P, P], BF16)
            part_max = sb(ph, "part_max", [P, TPB, 2, NBLK])
            row_max = sb(ph, "row_max", [P, TPB, 2])
            neg_r = sb(ph, "neg_r", [P, TPB, 2], F32R)
            neg = sb(ph, "neg", [P, TPB, 2, 2])
            rden = sb(ph, "rden", [P, DCH])
            oT = sb(ph, "oT", [P, BLK])
            oT_hi = sb(ph, "oT_hi", [P, BLK], F32R)
            oT_lo = sb(ph, "oT_lo", [P, BLK], F32R)
            for e in ("sync", "tensor", "vector", "scalar", "gpsimd"):
                need(e, before)
            bank_free.clear()
            kd_ok = split_weights("kd", w_raw[:, 0:CH * RANK].rearrange("p (h r) -> p h r", h=CH), kd_hi[:, :, :], kd_lo[:, :, :], wKD)
            t = [do("gpsimd", "att_fill", lambda e: e.memset(pick[:, :, :, :], 0.0)),
                 do("gpsimd", "att_fill", lambda e: e.memset(sel[:, :, :], 1.0)),
                 do("gpsimd", "att_fill", lambda e: e.memset(maskQ[:, :], 0.0)),
                 do("gpsimd", "att_fill", lambda e: e.memset(maskK[:, :], 0.0))]
            need("gpsimd", t)
            for c in range(DSUB):
                do("gpsimd", "att_const", lambda e: e.memset(pick[:, c, :, c], 1.0))
            do("gpsimd", "att_const", lambda e: e.affine_select(
                out=sel[:, 0, :], in_=sel[:, 0, :], compare_op=ALU.is_ge, fill=0.0, base=DH + 1,
                pattern=[[0, BLK]], channel_multiplier=-1))
            do("gpsimd", "att_const", lambda e: e.affine_select(
                out=sel[:, 1, :], in_=sel[:, 1, :], compare_op=ALU.is_ge, fill=0.0, base=-(DH + 2),
                pattern=[[0, BLK]], channel_multiplier=1))
            do("gpsimd", "att_const", lambda e: e.affine_select(
                out=maskQ[:, :], in_=maskQ[:, :], compare_op=ALU.is_ge, fill=MASKED, base=0,
                pattern=[[-1, P]], channel_multiplier=1))
            const_ok = do("gpsimd", "att_const", lambda e: e.affine_select(
                out=maskK[:, :], in_=maskK[:, :], compare_op=ALU.is_ge, fill=MASKED, base=0,
                pattern=[[1, P]], channel_multiplier=-1))
            need("vector", const_ok)
            for i in range(NK):
                for h in range(2):
                    sel_ok = do("vector", "sel_rows", lambda e, i=i, h=h: e.tensor_copy(
                        kB[i][h][DH:DH + 4, :], sel[DH:DH + 4, h, :]))
            w_ok, w_free = {}, [None, None]

            def load_pair(n):
                s = n % 2
                w_ok[n] = split_weights("wP", w_raw[:, :], w_hi[s][:, :], w_lo[s][:, :], wPair[n % NPAIR],
                                        free=[w_free[s], w_ok.get(n - 1, kd_ok)])

            def wp(n, a, z):
                return (w_hi[n % 2][:, a:z], w_lo[n % 2][:, a:z])

            kv_free, q_free, prob_free = [None] * NK, [None, None], [None] * NPROB
            score_free, xn_free = [None] * NSCORE, [None, None]
            acc_free = [sel_ok, None]
            free = dict.fromkeys(("part", "neg", "rden", "oT", "xT", "lat", "out"))
            q_ok, k_ok, v_ok, m_ok, lat_ok, batch_rstd = {}, {}, {}, {}, {}, {}
            t_of = {"step": 0}
            units = [(b, p, j) for b in range(NB) for p in range(NPAIR) for j in range(NBLK)]

            def prepare_sequence(b):
                def statistics(j):
                    for k in range(b * NT + j * TPB, b * NT + (j + 1) * TPB):
                        tile_stats(k, X[:, k, :], X_done[k])
                    if j == NBLK - 1:
                        batch_rstd[b] = inverse_std(b * NT, (b + 1) * NT)

                def normal(t):
                    s, k = t % 2, b * NT + t
                    need("vector", batch_rstd[b], xn_free[s])
                    normal_ok[t] = normalise(xn[s][:, :], X[:, k, :], k, "att_xn")

                def turn_tile(t):
                    s = t % 2
                    if t == 0:
                        normal(0)
                    if t + 1 < NT:
                        normal(t + 1)
                    n, ps = bank_pair()
                    need("tensor", normal_ok[t], ident_ok)
                    run("tensor", lambda e: e.transpose(ps[:, 0, 0:P], xn[s][:, 0:P], ident[:, :]))
                    done = do("tensor", "att_turned", lambda e: e.transpose(ps[:, 1, 0:P], xn[s][:, P:C], ident[:, :]))
                    xn_free[s] = done
                    both, cols = ps[:, :, 0:P], slice(t * P, (t + 1) * P)
                    need("scalar", done, free["xT"])
                    hi = do("scalar", "att_xT_hi", lambda e: e.activation(xT_hi[:, :, cols], both, ACT.Copy))
                    need("vector", hi, done)
                    lo = do("vector", "att_xT_lo", lambda e: e.tensor_tensor(xT_lo[:, :, cols], both, xT_hi[:, :, cols], ALU.subtract))
                    bank_free[n] = [hi, lo]
                    turned_ok[t] = lo

                def latent(j):
                    cols = slice(j * BLK, (j + 1) * BLK)
                    n, ps = bank_pair()
                    ps = ps[:, 0, :]
                    need("tensor", turned_ok[(j + 1) * TPB - 1], kd_ok)
                    pairs = []
                    for c in range(CH):
                        pairs += terms((kd_hi[:, c, :], kd_lo[:, c, :]), (xT_hi[:, c, cols], xT_lo[:, c, cols]))
                    t = do("tensor", "latent", product(ps, pairs))
                    need("scalar", t, free["lat"])
                    hi = do("scalar", "lat_hi", lambda e: e.activation(lat_hi[:, cols], ps, ACT.Copy))
                    need("vector", hi, t)
                    lat_ok[b, j] = do("vector", "lat_lo", lambda e: e.tensor_tensor(lat_lo[:, cols], ps, lat_hi[:, cols], ALU.subtract))
                    bank_free[n] = [hi, lat_ok[b, j]]

                turned_ok, normal_ok = {}, {}
                pieces = [lambda j=j: statistics(j) for j in range(NBLK)]
                for j in range(NBLK):
                    pieces += [lambda t=t: turn_tile(t) for t in range(j * TPB, (j + 1) * TPB)]
                    pieces.append(lambda j=j: latent(j))
                return pieces

            def slot_of(n, j):
                return (n * NBLK + j) % NK

            def prepare(idx):
                b, p, j = units[idx]
                n = b * NPAIR + p
                qs, ks = (n * NBLK + j) % 2, slot_of(n, j)
                cols = slice(j * BLK, (j + 1) * BLK)
                u_ = (n, j)
                pieces = []

                def query():
                    need("tensor", w_ok[n], lat_ok[b, j])
                    bn, ps = bank_pair()
                    ps = ps[:, 0, :]
                    pairs = []
                    for c in range(CH):
                        pairs += terms(wp(n, c * P, (c + 1) * P), (xT_hi[:, c, cols], xT_lo[:, c, cols]))
                    done = do("tensor", "q_proj", product(ps, pairs))
                    free["xT"] = done
                    readers, dup = [], []
                    for h in range(2):
                        hi_, lo_ = slice(h * DH, (h + 1) * DH), slice((1 - h) * DH, (2 - h) * DH)
                        need("scalar", done, q_free[qs])
                        hi = do("scalar", "q_hi", lambda e, h=h, hi_=hi_: e.activation(
                            qA[qs][h][hi_, :], ps[hi_, :], ACT.Copy, scale=DH ** -0.5))
                        need("vector", hi, done, q_free[qs])
                        lo = do("vector", "q_lo", lambda e, h=h, hi_=hi_, lo_=lo_: e.scalar_tensor_tensor(
                            out=qA[qs][h][lo_, :], in0=ps[hi_, :], scalar=DH ** -0.5, in1=qA[qs][h][hi_, :],
                            op0=ALU.mult, op1=ALU.subtract))
                        need("sync", hi, q_free[qs])
                        dup.append(dma(f"qB_in{qs}{h}", qB[qs][h][0:DH, :].bitcast(F32), qA[qs][h][hi_, :].bitcast(F32)))
                        readers += [hi, lo]
                    bank_free[bn] = readers
                    q_ok[u_] = (readers, dup)

                def key():
                    bn, ps = bank_pair()
                    ps = ps[:, 0, :]
                    need("tensor", w_ok[n], lat_ok[b, j])
                    done = do("tensor", "k_proj", product(ps, terms(wp(n, 2 * P, 3 * P), (lat_hi[:, cols], lat_lo[:, cols]))))
                    readers, dup = [], []
                    for h in range(2):
                        hi_, lo_ = slice(h * DH, (h + 1) * DH), slice((1 - h) * DH, (2 - h) * DH)
                        need("scalar", done, kv_free[ks])
                        hi = do("scalar", "k_hi", lambda e, h=h, hi_=hi_: e.activation(kA[ks][h][hi_, :], ps[hi_, :], ACT.Copy))
                        need("vector", hi, done, kv_free[ks])
                        lo = do("vector", "k_lo", lambda e, h=h, hi_=hi_: e.tensor_tensor(
                            kB[ks][h][0:DH, :], ps[hi_, :], kA[ks][h][hi_, :], ALU.subtract))
                        need("sync", hi, kv_free[ks])
                        dup.append(dma(f"kA_in{ks}{h}", kA[ks][h][lo_, :].bitcast(F32), kA[ks][h][hi_, :].bitcast(F32)))
                        readers += [hi, lo]
                    bank_free[bn] = readers
                    k_ok[u_] = (readers, dup)

                def value():
                    bn, ps = bank_pair()
                    ps = ps[:, 0, :]
                    need("tensor", w_ok[n], lat_ok[b, j])
                    for t in range(TPB):
                        tc = slice(j * BLK + t * P, j * BLK + (t + 1) * P)
                        last = product(ps[:, t * P:(t + 1) * P], terms((lat_hi[:, tc], lat_lo[:, tc]), wp(n, 3 * P, 4 * P)))
                        if t < TPB - 1:
                            run("tensor", last)
                    done = do("tensor", "v_proj", last)
                    free["lat"] = done
                    need("scalar", done, kv_free[ks])
                    v_ok[u_] = do("scalar", "v_out", lambda e: e.activation(
                        V[ks][:, :, :], ps.rearrange("p (t d) -> p t d", d=P), ACT.Copy))
                    bank_free[bn] = [v_ok[u_]]

                maxima = []

                def maximum(t, c):
                    bn, ps = bank_pair()
                    need("tensor", q_ok[u_][0], k_ok[n, c][0], k_ok[n, c][1], const_ok)
                    diag = c == j
                    width = (t + 1) * P if diag else BLK
                    for h in range(2):
                        last = product(ps[:, h, 0:width], [(qA[qs][h][:, t * P:(t + 1) * P], kA[slot_of(n, c)][h][:, 0:width])], last=not diag)
                        if diag:
                            run("tensor", last)
                            last = lambda e: e.matmul(ps[:, h, t * P:width], ident16[:, :], maskQ[:, :], start=False, stop=True)
                        if h == 0:
                            run("tensor", last)
                    done = do("tensor", "q_dot_k", last)
                    need("vector", done, free["part"])
                    r = do("vector", "part_max", lambda e: e.reduce_max(part_max[:, t, :, c:c + 1], ps[:, :, 0:width], AX.X))
                    bank_free[bn] = [r]
                    maxima.append(r)

                neg_ok = []

                def minus_max():
                    need("vector", maxima[-1], free["neg"])
                    t = do("vector", "row_max", lambda e: e.reduce_max(row_max[:, :, :], part_max[:, :, :, 0:j + 1], AX.X))
                    free["part"] = t
                    need("vector", t)
                    t = do("vector", "neg_hi", lambda e: e.tensor_scalar(neg_r[:, :, :], row_max[:, :, :], -1.0, None, ALU.mult))
                    need("vector", t)
                    do("vector", "neg", lambda e: e.tensor_copy(neg[:, :, :, 0], neg_r[:, :, :].bitcast(F32)))
                    neg_ok.append(do("vector", "neg", lambda e: e.scalar_tensor_tensor(
                        out=neg[:, :, :, 1], in0=row_max[:, :, :], scalar=-1.0,
                        in1=neg_r[:, :, :].bitcast(F32), op0=ALU.mult, op1=ALU.subtract)))

                def turn_max():
                    bn, ps = bank_pair()
                    ps = ps[:, 0, :]
                    need("tensor", neg_ok[0], ident_ok)
                    for tt in range(TPB):
                        f = lambda e: e.transpose(ps[0:4, tt * P:(tt + 1) * P],
                                                  neg[:, tt, :, :].rearrange("p a b -> p (a b)"), ident[:, :])
                        if tt < TPB - 1:
                            run("tensor", f)
                    done = do("tensor", "neg_turned", f)
                    free["neg"] = done
                    need("scalar", done, q_free[qs])
                    for h in range(2):
                        m_ok[u_] = do("scalar", "neg_rows", lambda e: e.activation(qB[qs][h][DH:DH + 4, :], ps[0:4, :], ACT.Copy))
                    bank_free[bn] = [m_ok[u_]]

                pieces = prepare_sequence(b) if (p, j) == (0, 0) else []
                pieces += [key, query, value]
                for c in range(j + 1):
                    pieces += [lambda t=t, c=c: maximum(t, c) for t in range(TPB)]
                pieces += [minus_max, turn_max]
                if j == 2 and n + 1 < NB * NPAIR:
                    pieces.append(lambda: load_pair(n + 1))
                return pieces

            def finish(idx, done, total):
                b, p, j = units[idx]
                n, os_ = b * NPAIR + p, idx % 2
                st = {}

                def take_out():
                    need("scalar", done, free["oT"])
                    st["out"] = free["out"] = do("scalar", "oT_raw", lambda e: e.activation(oT[:, :], heads_out[:, :], ACT.Copy))

                def sums():
                    if "accV" not in total:
                        st["sum"] = total["accG"][-1]
                        return
                    need("gpsimd", total["accG"], total["accV"])
                    st["sum"] = do("gpsimd", "acc_sum", lambda e: e.tensor_tensor(
                        accG[os_][:, :, :], accG[os_][:, :, :], accV[os_][:, :, :], ALU.add))

                def denominators():
                    bn, ps = bank_pair()
                    need("tensor", st["sum"], total["accG"], const_ok)
                    for c in range(DSUB):
                        for g in range(4):
                            x = (g % 2 * DSUB + c) * DCH
                            f = lambda e: e.matmul(ps[g * QUAD:(g + 1) * QUAD, 0, 0:DCH], pick[:, c, :, :].rearrange("p a b -> p (a b)"),
                                                   accG[os_][:, g // 2, x:x + DCH], start=(c == 0), stop=(c == DSUB - 1))
                            if (c, g) != (DSUB - 1, 3):
                                run("tensor", f)
                    t = do("tensor", "denominator", f)
                    acc_free[os_] = [st["sum"], t]
                    need("vector", t, free["rden"])
                    st["r"] = do("vector", "rden", lambda e: e.reciprocal(rden[:, :], ps[:, 0, 0:DCH]))
                    bank_free[bn] = [st["r"]]

                def divide():
                    bn, ps = bank_pair()
                    need("tensor", st["r"], ident_ok)
                    for x in range(BLK // DCH):
                        for h in range(2):
                            row = (2 * h + x // DSUB) * QUAD + x % DSUB
                            f = lambda e: e.matmul(ps[h * DH:(h + 1) * DH, 0, x * DCH:(x + 1) * DCH],
                                                   ident[:, row:row + 1].broadcast_to([P, DH]), rden[:, :], start=True, stop=True)
                            if (x, h) != (BLK // DCH - 1, 1):
                                run("tensor", f)
                    t = free["rden"] = do("tensor", "inverses", f)
                    need("vector", t, st["out"])
                    st["o"] = do("vector", "oT", lambda e: e.tensor_tensor(oT[:, :], oT[:, :], ps[:, 0, :], ALU.mult))
                    bank_free[bn] = [st["o"]]

                def two_parts():
                    need("scalar", st["o"], free["oT"])
                    hi = do("scalar", "oT_hi", lambda e: e.activation(oT_hi[:, :], oT[:, :], ACT.Copy))
                    need("gpsimd", hi, st["o"], free["oT"])
                    st["lo"] = do("gpsimd", "oT_lo", lambda e: e.tensor_tensor(oT_lo[:, :], oT[:, :], oT_hi[:, :], ALU.subtract))

                def project():
                    bn, ps = bank_pair()
                    need("tensor", st["lo"])
                    for t in range(TPB):
                        cs = slice(t * P, (t + 1) * P)
                        y = do("tensor", "att_y", product(ps[:, t // 2, (t % 2) * C:(t % 2 + 1) * C],
                               terms((oT_hi[:, cs], oT_lo[:, cs]), wp(n, 4 * P, 4 * P + C))))
                    k = b * NT + j * TPB
                    need("vector", y, *(X_done[k + t] for t in range(TPB)))
                    x = [do("vector", "x_plus_att", lambda e: e.tensor_tensor(
                        X[:, k:k + TPB, :], X[:, k:k + TPB, :], ps[:, :, :].rearrange("p a (t c) -> p (a t) c", c=C), ALU.add))]
                    for t in range(TPB):
                        X_done[k + t] = x
                    bank_free[bn] = x
                    free["oT"] = [y, st["lo"]]
                    w_free[n % 2] = y

                take_out()
                return [sums, None, denominators, None, divide, two_parts, None, None, project]

            def weave(first, second):
                tagged = [((i + 0.5) / len(first), i, f) for i, f in enumerate(first)]
                tagged += [((i + 0.5) / len(second), i, f) for i, f in enumerate(second)]
                return [x[-1] for x in sorted(tagged, key=lambda x: x[:2])]

            load_pair(0)
            for f in prepare(0):
                f()
            def run_unit(idx, end_of_last):
                b, p, j = units[idx]
                n = b * NPAIR + p
                u_ = (n, j)
                qs = os_ = idx % 2
                nk = TPB * (j + 1)

                def score(t):
                    pr = t_of["step"] % NPROB
                    c, tt = divmod(t, TPB)
                    x0 = tt * P if c == j else 0
                    ks = slot_of(n, c)
                    kc = slice(tt * P, (tt + 1) * P)
                    for h in range(2):
                        st = (2 * t_of["step"] + h) % NSCORE
                        need("tensor", score_free[st], q_ok[u_][0], q_ok[u_][1], m_ok[u_], k_ok[n, c][0], k_ok[n, c][1], sel_ok, const_ok)
                        run("tensor", product(scores[:, st, x0:], [(kA[ks][h][:, kc], qA[qs][h][:, x0:])], last=False))
                        if c == j:
                            run("tensor", lambda e: e.matmul(scores[:, st, x0:x0 + P], ident16[:, :], maskK[:, :], start=False, stop=False))
                        done = do("tensor", "score", product(scores[:, st, x0:], [(kB[ks][h][:, kc], qB[qs][h][:, x0:])], first=False))
                        need("scalar", done, prob_free[pr])
                        score_free[st] = e_ok = do("scalar", "exp", lambda e: e.activation(prob[pr][:, h, x0:], scores[:, st, x0:], ACT.Exp))
                    t_of["step"] += 1
                    return pr, x0, e_ok

                total = {}

                def weigh(t, pr, x0, e_ok):
                    c, tt = divmod(t, TPB)
                    need("tensor", e_ok, v_ok[n, c])
                    if t == 0:
                        need("tensor", free["out"])
                    for h in range(2):
                        f = lambda e: e.matmul(heads_out[h * DH:(h + 1) * DH, x0:],
                                               V[slot_of(n, c)][:, tt, h * DH:(h + 1) * DH], prob[pr][:, h, x0:],
                                               start=(t == 0), stop=(t == nk - 1))
                        if h == 0:
                            run("tensor", f)
                    done = do("tensor", "weigh", f)
                    prob_free[pr] = [done]
                    return done

                def accumulate(t, cur, before):
                    _, pr, x0, e_ok = cur
                    if t == 0:
                        return
                    if t == 1:
                        _, pr0, _, e0 = before
                        need("gpsimd", e_ok, e0, acc_free[os_])
                        a = [do("gpsimd", "accG", lambda e: e.tensor_tensor(
                            accG[os_][:, :, x0:], prob[pr0][:, :, x0:], prob[pr][:, :, x0:], ALU.add))]
                        if x0:
                            a.append(do("gpsimd", "accG", lambda e: e.tensor_copy(accG[os_][:, :, 0:x0], prob[pr0][:, :, 0:x0])))
                        total["accG"] = a
                        prob_free[pr0].append(a[-1])
                    elif t % VSHARE[j] == 2:
                        need("vector", e_ok, acc_free[os_], total.get("accV"))
                        if t == 2:
                            a = [do("vector", "accV", lambda e: e.tensor_copy(accV[os_][:, :, x0:], prob[pr][:, :, x0:]))]
                            if x0:
                                a.append(do("vector", "accV", lambda e: e.memset(accV[os_][:, :, 0:x0], 0.0)))
                        else:
                            a = [do("vector", "accV", lambda e: e.tensor_tensor(
                                accV[os_][:, :, x0:], accV[os_][:, :, x0:], prob[pr][:, :, x0:], ALU.add))]
                        total["accV"] = a
                    else:
                        need("gpsimd", e_ok, total["accG"])
                        a = [do("gpsimd", "accG", lambda e: e.tensor_tensor(
                            accG[os_][:, :, x0:], accG[os_][:, :, x0:], prob[pr][:, :, x0:], ALU.add))]
                        total["accG"] = a
                    prob_free[pr].append(a[-1])

                cost = [BLK + P - max(0, t - TPB * j) * P for t in range(nk)]
                upto = [sum(cost[:t + 1]) / sum(cost) for t in range(nk)]
                fill = given = None
                prev = before = None
                for t in range(nk):
                    cur, last = (t,) + score(t), prev
                    if t == 0:
                        rest = end_of_last() if end_of_last else []
                        ahead = prepare(idx + 1) if idx + 1 < len(units) else []
                        fill, given = weave(ahead, rest), 0
                    want = min(len(fill), int(len(fill) * upto[t] / 0.95))
                    half = (given + want) // 2
                    while given < want or prev is not None:
                        if given >= half and prev is not None:
                            weigh(*prev)
                            accumulate(t - 1, prev, before)
                            prev = None
                        if given < want:
                            if fill[given]:
                                fill[given]()
                            given += 1
                    prev, before = cur, last

                def end():
                    done = weigh(*prev)
                    accumulate(nk - 1, prev, before)
                    q_free[qs] = done
                    if j == NBLK - 1:
                        for c in range(NBLK):
                            kv_free[slot_of(n, c)] = done
                    return finish(idx, done, total)

                return end

            end = None
            for idx in range(len(units)):
                end = run_unit(idx, end)
            rest = end()
            for f in rest:
                if f:
                    f()

        bank_free.clear()
        channel_mixer("b", True, pg.everything_so_far())


def kernel(L0_attn_a_u, L0_attn_a_A_diag, L0_attn_a_Bmat, L0_attn_a_Cmat, L0_attn_a_Dmat, L0_attn_a_h0,
           L0_attn_a_ln_gamma, L0_attn_a_ln_beta, L0_attn_b_w_kv_down, L0_attn_b_w_kv_up, L0_attn_b_w_q,
           L0_attn_b_w_out, L0_ffn_W_r, L0_ffn_W_k, L0_ffn_W_v, L0_ffn_mu_r, L0_ffn_mu_k):
    import numpy as np
    import concourse.bacc as bacc
    from concourse.bass_utils import run_bass_kernel_spmd

    def halves(w):
        return np.asarray(w).reshape(CH, P, -1).transpose(1, 0, 2)

    def cols(v):
        return np.asarray(v).reshape(CH, P).T

    wq, up, wo = np.asarray(L0_attn_b_w_q), np.asarray(L0_attn_b_w_kv_up), np.asarray(L0_attn_b_w_out)
    HD = NH * DH
    pair = [np.concatenate([halves(wq[:, i:i + P]).reshape(P, CH * P), up[:, i:i + P], up[:, HD + i:HD + i + P],
                            wo[i:i + P, :]], axis=1) for i in range(0, HD, P)]
    arrays = {
        "u": np.asarray(L0_attn_a_u).reshape(NB * T, C),
        "wA": np.stack([halves(np.asarray(w).T) for w in (L0_attn_a_Bmat, L0_attn_a_Cmat, L0_attn_a_Dmat)], axis=1),
        "wF": np.stack([halves(np.asarray(w).T) for w in (L0_ffn_W_r, L0_ffn_W_k, L0_ffn_W_v)], axis=1),
        "wKD": halves(L0_attn_b_w_kv_down),
        "wPair": np.stack(pair),
        "aDiag": cols(L0_attn_a_A_diag),
        "h0": cols(L0_attn_a_h0),
        "gb": np.broadcast_to(np.stack([np.asarray(L0_attn_a_ln_gamma), np.asarray(L0_attn_a_ln_beta)])[None], (P, 2, C)),
        "mu": np.stack([cols(L0_ffn_mu_r), cols(L0_ffn_mu_k)], axis=1),
    }
    arrays = {k: np.ascontiguousarray(v) for k, v in arrays.items()}
    nc = bacc.Bacc("TRN2", target_bir_lowering=False, num_devices=1)
    args = [nc.dram_tensor(k, v.shape, mybir.dt.from_np(v.dtype), kind="ExternalInput").ap() for k, v in arrays.items()]
    out = nc.dram_tensor("out", (NB * T, C), F32, kind="ExternalOutput").ap()
    build(nc, *args, out)
    r = run_bass_kernel_spmd(nc, [arrays], core_ids=[0])
    return r.results[0]["out"].reshape(NB, T, C)
```

```python
from contextlib import ExitStack

import concourse.bass as bass
from concourse import mybir

ALU = mybir.AluOpType
ACT = mybir.ActivationFunctionType
AX = mybir.AxisListType
F32 = mybir.dt.float32
F32R = mybir.dt.float32r
BF16 = mybir.dt.bfloat16

P = 128
NB, T, C = 2, 2048, 256
CH = C // P
BLK = 512
NBLK = T // BLK
TPB = BLK // P
NT = T // P
NH, DH = 16, 64
NPAIR = NH // 2
RANK = 128
EPS = 1e-5
CLAMP = 1e6
MASKED = -3.0e38
WPC = 2 * P + P + P + C
NSCORE = 3
QUAD = 32
DSUB = 2
DCH = 2 * BLK // (4 * DSUB)
STATS_BEFORE = {(0, 1, 0): 1, (1, 2, 0): 0}
NPROB = 4
NK = NBLK + 1


class Program:

    def __init__(self, nc, ctx):
        self.nc, self.ctx = nc, ctx
        self.engine = {"tensor": nc.tensor, "vector": nc.vector, "scalar": nc.scalar,
                       "gpsimd": nc.gpsimd, "sync": nc.sync}
        self.sems, self.value, self.waited = {}, {}, {}

    def do(self, engine, step, make):
        return self._signal(engine, step, make, 1)

    def dma(self, step, out, in_):
        return self._signal("sync", step, lambda e: e.dma_start(out, in_), 16)

    def _signal(self, engine, step, make, by):
        if step not in self.sems:
            self.sems[step] = self.ctx.enter_context(self.nc.semaphore(step))
            self.value[step] = 0
        self.value[step] += by
        sem = self.sems[step]
        make(self.engine[engine]).then_inc(sem, by)
        return step, self.value[step]

    def run(self, engine, make):
        make(self.engine[engine])

    def need(self, engine, *done):
        for d in done:
            if d is None:
                continue
            if isinstance(d, list):
                self.need(engine, *d)
                continue
            step, value = d
            if self.waited.get((engine, step), 0) < value:
                self.waited[engine, step] = value
                self.engine[engine].wait_ge(self.sems[step], value)

    def everything_so_far(self):
        return [(s, v) for s, v in self.value.items()]


def build(nc, u, wA, wF, wKD, wPair, aDiag, h0, gb, mu, out):
    ctx = ExitStack()
    with ctx:
        pg = Program(nc, ctx)
        do, dma, run, need = pg.do, pg.dma, pg.run, pg.need

        def sb(where, name, shape, dt=F32):
            return where.enter_context(nc.sbuf_tensor(name, shape, dt))

        scores = ctx.enter_context(nc.psum_tensor("scores", [P, NSCORE, BLK], F32))
        heads_out = ctx.enter_context(nc.psum_tensor("heads_out", [P, BLK], F32))
        work = [ctx.enter_context(nc.psum_tensor(f"work{i}", [P, 2, BLK], F32)) for i in range(2)]
        banks = ([scores[:, i, :] for i in range(NSCORE)] + [heads_out[:, :]]
                 + [w[:, i, :] for w in work for i in range(2)])
        bank_free = {}
        turn = {"next": 0}

        def bank():
            n = turn["next"] % len(banks)
            turn["next"] += 1
            need("tensor", bank_free.get(n))
            return n, banks[n]

        def one_bank():
            n = turn["next"] % 4
            turn["next"] += 1
            need("tensor", bank_free.get(n))
            return (n,), work[n // 2][:, n % 2, :]

        def two_banks():
            turn["next"] += turn["next"] % 2
            n = turn["next"] % 4
            turn["next"] += 2
            need("tensor", bank_free.get(n), bank_free.get(n + 1))
            return (n, n + 1), work[n // 2]

        def release(taken, readers):
            for n in taken:
                bank_free[n] = readers

        X = sb(ctx, "X", [P, NB * NT, C])
        ident = sb(ctx, "ident", [P, P])
        ident16 = sb(ctx, "ident16", [P, P], BF16)
        mean_var = sb(ctx, "mean_var", [P, NB * NT, 2])
        stats = sb(ctx, "stats", [P, 4, 6])
        std = sb(ctx, "std", [P, NB * NT])
        rstd = sb(ctx, "rstd", [P, NB * NT])

        X_done = {}

        def load_x(i):
            loaded = dma(f"x_in{i}", X[:, i * TPB:(i + 1) * TPB, :],
                         u[i * BLK:(i + 1) * BLK, :].rearrange("(t p) c -> p t c", p=P))
            for k in range(i * TPB, (i + 1) * TPB):
                X_done[k] = [loaded]

        load_x(0)

        z = [do("gpsimd", "ident_zero", lambda e: e.memset(ident[:, :], 0.0)),
             do("gpsimd", "ident_zero", lambda e: e.memset(ident16[:, :], 0.0))]
        need("gpsimd", z)
        for m in (ident, ident16):
            ident_ok = do("gpsimd", "ident", lambda e, m=m: e.affine_select(
                out=m[:, :], in_=m[:, :], compare_op=ALU.not_equal, fill=1.0, base=0,
                pattern=[[-1, P]], channel_multiplier=1))

        stats_free = [None] * 4
        norm_free = {"last": None}

        def tile_stats(k, src, ready):
            slot = k % 4
            need("vector", ready, stats_free[slot], norm_free["last"])
            need("vector", do("vector", "bn_stats", lambda e: e.bn_stats(stats[:, slot, :], src)))
            stats_free[slot] = do("vector", "bn_aggr", lambda e: e.bn_aggr(mean_var[:, k, :], stats[:, slot, :]))

        def inverse_std(a, z):
            need("vector", *stats_free)
            t = do("vector", "var_eps", lambda e: e.tensor_scalar(std[:, a:z], mean_var[:, a:z, 1], EPS, None, ALU.add))
            need("scalar", t)
            t = do("scalar", "std", lambda e: e.activation(std[:, a:z], std[:, a:z], ACT.Sqrt))
            need("vector", t)
            return do("vector", "rstd", lambda e: e.reciprocal(rstd[:, a:z], std[:, a:z]))

        seq_rstd = {}

        def stats_pieces(b, parts):
            def piece(i):
                for k in range(b * NT + i * NT // parts, b * NT + (i + 1) * NT // parts):
                    tile_stats(k, X[:, k, :], X_done[k])
                if i == parts - 1:
                    seq_rstd[b] = inverse_std(b * NT, (b + 1) * NT)
            return [lambda i=i: piece(i) for i in range(parts)]

        def normalise(dst, src, k, step):
            norm_free["last"] = do("vector", step, lambda e: e.tensor_scalar(
                dst, src, mean_var[:, k, 0:1], rstd[:, k:k + 1], ALU.subtract, ALU.mult))
            return norm_free["last"]

        def terms(a, b):
            return [(a[0], b[0]), (a[0], b[1]), (a[1], b[0])]

        def product(dst, pairs, first=True, last=True):
            made = []
            for n, (l, r) in enumerate(pairs):
                made.append(lambda e, l=l, r=r, s=(first and n == 0), z=(last and n == len(pairs) - 1):
                            e.matmul(dst, l, r, start=s, stop=z))
            for m in made[:-1]:
                run("tensor", m)
            return made[-1]

        def split_weights(name, raw, hi, lo, src, free=None, loaded=None):
            need("sync", free)
            need("vector", loaded or dma(f"{name}_in", raw, src), free)
            t = do("vector", f"{name}_hi", lambda e: e.tensor_copy(hi, raw))
            need("vector", t)
            return do("vector", f"{name}_lo", lambda e: e.tensor_tensor(lo, raw, hi, ALU.subtract))

        def transposed_tiles(k0, xn_of, ready):
            res = []
            for h in range(CH):
                n, ps = bank()
                for t in range(TPB):
                    need("tensor", ready[t], ident_ok)
                    f = lambda e, t=t, h=h, ps=ps: e.transpose(
                        ps[:, t * P:(t + 1) * P], xn_of(t)[:, h * P:(h + 1) * P], ident[:, :])
                    if t < TPB - 1:
                        run("tensor", f)
                done = do("tensor", "x_turned", f)
                res.append((n, ps, done))
            return res

        def mixer_weights_memory(where, tag):
            return [sb(where, f"wF_raw{tag}", [P, 3, CH, C]), sb(where, f"wF_hi{tag}", [P, 3, CH, C], F32R),
                    sb(where, f"wF_lo{tag}", [P, 3, CH, C], F32R), sb(where, f"mu{tag}", [P, 2, CH]),
                    sb(where, f"one_mu{tag}", [P, 2, CH])]

        def load_mixer_weights(w_raw, w_hi, w_lo, mu_sb, one_mu):
            return dma("mu_in", mu_sb[:, :, :], mu), dma("wF_in", w_raw[:, :, :, :], wF)

        def split_mixer_weights(w_raw, w_hi, w_lo, mu_sb, one_mu, mu_in, wF_in):
            w_ok = split_weights("wF", w_raw[:, :, :, :], w_hi[:, :, :, :], w_lo[:, :, :, :], wF, loaded=wF_in)
            need("vector", mu_in)
            mu_ok = do("vector", "one_minus_mu", lambda e: e.tensor_scalar(one_mu[:, :, :], mu_sb[:, :, :], -1.0, 1.0, ALU.mult, ALU.add))
            return w_hi, w_lo, mu_sb, one_mu, w_ok, mu_ok

        tail_scope = ctx.enter_context(ExitStack())
        gamma_beta = sb(tail_scope, "gamma_beta", [P, 2, C])
        G = sb(tail_scope, "G", [P, NB * NT, C])
        nrm = sb(tail_scope, "nrm", [P, 2, 2, C])
        clp = sb(tail_scope, "clp", [P, 2, 2, C])
        msk = sb(tail_scope, "msk", [P, 2, 2, C])
        fin = sb(tail_scope, "fin", [P, 2, 2, C], mybir.dt.uint32)
        first_mixer_memory = mixer_weights_memory(tail_scope, "a")
        G_done, act_rstd, beta_ok = {}, {}, {}
        nrm_free, tail_free = [None, None], [None, None]

        def tail_norm(k):
            s = (k // 2) % 2
            need("vector", act_rstd[k // NT], nrm_free[s])
            for q in range(2):
                t = normalise(nrm[:, s, q, :], G[:, k + q, :], k + q, "act_norm")
            need("gpsimd", t, small_in)
            both = [gamma_beta[:, i:i + 1, :].broadcast_to([P, 2, C]) for i in range(2)]
            t = do("gpsimd", "act_gamma", lambda e: e.tensor_tensor(nrm[:, s, :, :], nrm[:, s, :, :], both[0], ALU.mult))
            need("gpsimd", t)
            beta_ok[k] = do("gpsimd", "act_beta", lambda e: e.tensor_tensor(nrm[:, s, :, :], nrm[:, s, :, :], both[1], ALU.add))

        def tail_add(k):
            s = (k // 2) % 2
            need("vector", beta_ok[k], tail_free[s])
            t = do("vector", "clamp", lambda e: e.tensor_scalar(clp[:, s, :, :], nrm[:, s, :, :], -CLAMP, CLAMP, ALU.max, ALU.min))
            m = do("vector", "not_nan", lambda e: e.tensor_tensor(msk[:, s, :, :], nrm[:, s, :, :], nrm[:, s, :, :], ALU.is_equal))
            f = do("vector", "is_finite", lambda e: e.tensor_scalar(fin[:, s, :, :], nrm[:, s, :, :], 0.0, 0.0, ALU.mult, ALU.is_equal))
            need("vector", t, m)
            t = do("vector", "no_nan", lambda e: e.tensor_tensor(clp[:, s, :, :], clp[:, s, :, :], msk[:, s, :, :], ALU.mult))
            need("vector", t, f)
            t = do("vector", "nan_to_num", lambda e: e.copy_predicated(clp[:, s, :, :], fin[:, s, :, :], nrm[:, s, :, :]))
            nrm_free[s] = t
            need("gpsimd", t)
            X_done[k] = X_done[k + 1] = [do("gpsimd", "x_plus_ssm", lambda e: e.tensor_tensor(
                X[:, k:k + 2, :], X[:, k:k + 2, :], clp[:, s, :, :], ALU.add))]
            tail_free[s] = X_done[k]

        def tail_pieces(b):
            ks = list(range(b * NT, (b + 1) * NT, 2))
            pieces = []
            for n, k in enumerate(ks):
                pieces.append(lambda k=k: tail_norm(k))
                if n:
                    pieces.append(lambda k=k: tail_add(k - 2))
            return pieces + [lambda: tail_add(ks[-1])]

        def spread(pieces, n):
            return [pieces[len(pieces) * i // n:len(pieces) * (i + 1) // n] for i in range(n)]

        with ExitStack() as ph:
            w_raw = sb(ph, "wA_raw", [P, 3, CH, C])
            w_hi = sb(ph, "wA_hi", [P, 3, CH, C], F32R)
            w_lo = sb(ph, "wA_lo", [P, 3, CH, C], F32R)
            a_in = sb(ph, "a_in", [P, CH])
            a_abs = sb(ph, "a_abs", [P, CH])
            a_log = sb(ph, "a_log", [P, CH])
            a_col = sb(ph, "a_col", [P, CH])
            zeros = sb(ph, "zeros", [P, BLK])
            decay = sb(ph, "decay", [P, CH, BLK])
            state0 = sb(ph, "state0", [P, CH])
            xn = sb(ph, "xn", [P, 2, TPB, C])
            xT_hi = sb(ph, "xT_hi", [P, 3, CH, BLK], F32R)
            xT_lo = sb(ph, "xT_lo", [P, 3, CH, BLK], F32R)
            xs = sb(ph, "xs", [P, 2, CH, BLK])
            xs_hi = sb(ph, "xs_hi", [P, 2, CH, BLK], F32R)
            xs_lo = sb(ph, "xs_lo", [P, 2, CH, BLK], F32R)
            small_in = dma("ssm_small_in", a_in[:, :], aDiag)
            small_in = dma("ssm_small_in", state0[:, :], h0)
            small_in = dma("ssm_small_in", gamma_beta[:, :, :], gb)
            load_x(1)
            wA_in = dma("wA_in", w_raw[:, :, :, :], wA)
            for i in range(2, NB * NBLK):
                load_x(i)
            xn_free, xT_free, xs_free = [None, None], [None] * 3, [None, None]
            scanned, turned_ok, ssm_rstd = {}, {}, {}

            def x_stats(i, z):
                for k in range(i * TPB, z * TPB):
                    tile_stats(k, X[:, k, :], X_done[k])
                ok = inverse_std(i * TPB, z * TPB)
                ssm_rstd.update((n, ok) for n in range(i, z))

            def ssm_front(i):
                s, x, k0 = i % 2, i % 3, i * TPB
                need("vector", ssm_rstd[i], xn_free[s])
                ready = [normalise(xn[:, s, t, :], X[:, k0 + t, :], k0 + t, "ssm_xn") for t in range(TPB)]
                turned = transposed_tiles(k0, lambda t: xn[:, s, t, :], ready)
                xn_free[s] = turned[-1][2]
                for h, (n, ps, done) in enumerate(turned):
                    need("scalar", done, xT_free[x])
                    hi = do("scalar", "ssm_xT_hi", lambda e: e.activation(xT_hi[:, x, h, :], ps, ACT.Copy))
                    need("vector", hi, done)
                    turned_ok[i] = do("vector", "ssm_xT_lo", lambda e: e.tensor_tensor(
                        xT_lo[:, x, h, :], ps, xT_hi[:, x, h, :], ALU.subtract))
                    bank_free[n] = [hi, turned_ok[i]]

            def ssm_states(i):
                s, x = i % 2, i % 3
                b, j = divmod(i, NBLK)
                need("tensor", turned_ok[i], wA_ok)
                for m in range(CH):
                    n, ps = bank()
                    pairs = []
                    for c in range(CH):
                        pairs += terms((w_hi[:, 0, c, m * P:(m + 1) * P], w_lo[:, 0, c, m * P:(m + 1) * P]),
                                       (xT_hi[:, x, c, :], xT_lo[:, x, c, :]))
                    bu = do("tensor", "bu", product(ps, pairs))
                    need("vector", bu, decay_ok, small_in, scanned.get((b, j - 1, m)), xs_free[s])
                    init = state0[:, m:m + 1] if j == 0 else xs[:, 1 - s, m, BLK - 1:BLK]
                    sc = do("vector", "scan", lambda e: e.tensor_tensor_scan(
                        xs[:, s, m, :], decay[:, m, :], ps, init, ALU.mult, ALU.add))
                    scanned[b, j, m] = sc
                    bank_free[n] = [sc]
                    need("scalar", sc, xs_free[s])
                    hi = do("scalar", "xs_hi", lambda e: e.activation(xs_hi[:, s, m, :], xs[:, s, m, :], ACT.Copy))
                    need("gpsimd", hi, sc, xs_free[s])
                    scanned[i, "parts"] = do("gpsimd", "xs_lo", lambda e: e.tensor_tensor(
                        xs_lo[:, s, m, :], xs[:, s, m, :], xs_hi[:, s, m, :], ALU.subtract))

            def ssm_output(i):
                s, x = i % 2, i % 3
                need("tensor", scanned[i, "parts"])
                for t in range(0, TPB, 2):
                    n, ps = bank()
                    for q in range(2):
                        cols = slice((t + q) * P, (t + q + 1) * P)
                        pairs = []
                        for c in range(CH):
                            pairs += terms((xT_hi[:, x, c, cols], xT_lo[:, x, c, cols]),
                                           (w_hi[:, 2, c, :], w_lo[:, 2, c, :]))
                        for c in range(CH):
                            pairs += terms((xs_hi[:, s, c, cols], xs_lo[:, s, c, cols]),
                                           (w_hi[:, 1, c, :], w_lo[:, 1, c, :]))
                        y = do("tensor", "ssm_y", product(ps[:, q * C:(q + 1) * C], pairs))
                    kk = i * TPB + t
                    need("scalar", y)
                    g = do("scalar", "gelu", lambda e: e.activation(
                        G[:, kk:kk + 2, :], ps.rearrange("p (t c) -> p t c", c=C), ACT.Gelu))
                    bank_free[n] = [g]
                    G_done[kk] = G_done[kk + 1] = g
                xT_free[x] = y
                xs_free[s] = [y, scanned[i, "parts"]]

            def ssm_stats(i):
                for k in range(i * TPB, (i + 1) * TPB):
                    tile_stats(k, G[:, k, :], G_done[k])

            nb = NB * NBLK
            x_stats(0, 1)
            ssm_front(0)
            zeros_ok = do("vector", "zeros", lambda e: e.memset(zeros[:, :], 0.0))
            need("vector", small_in)
            t = do("vector", "softplus_v", lambda e: e.tensor_scalar(a_abs[:, :], a_in[:, :], -1.0, None, ALU.mult))
            need("vector", t)
            t = do("vector", "softplus_v", lambda e: e.tensor_tensor(a_abs[:, :], a_abs[:, :], a_in[:, :], ALU.min))
            need("scalar", t)
            t = do("scalar", "softplus_a", lambda e: e.activation(a_log[:, :], a_abs[:, :], ACT.Exp))
            need("scalar", t)
            t = do("scalar", "softplus_a", lambda e: e.activation(a_log[:, :], a_log[:, :], ACT.Ln, bias=1.0))
            need("vector", t)
            t = do("vector", "softplus_v", lambda e: e.scalar_tensor_tensor(
                out=a_col[:, :], in0=a_in[:, :], scalar=0.0, in1=a_log[:, :], op0=ALU.max, op1=ALU.add))
            need("vector", t, zeros_ok)
            for h in range(CH):
                decay_ok = do("vector", "decay", lambda e, h=h: e.tensor_scalar(
                    decay[:, h, :], zeros[:, :], a_col[:, h:h + 1], None, ALU.subtract))

            wA_ok = split_weights("wA", w_raw[:, :, :, :], w_hi[:, :, :, :], w_lo[:, :, :, :], wA, loaded=wA_in)
            x_stats(1, NBLK)
            ssm_front(1)
            ssm_states(0)
            tail = spread(tail_pieces(0), NBLK - 1)
            for i in range(nb):
                if i == 0:
                    x_stats(NBLK, nb)
                if i == nb - 1:
                    for f in stats_pieces(0, 1):
                        f()
                if i == 1:
                    wF_in = load_mixer_weights(*first_mixer_memory)
                if i == 2:
                    mixer_weights = split_mixer_weights(*first_mixer_memory, *wF_in)
                if i + 2 < nb:
                    ssm_front(i + 2)
                if i + 1 < nb:
                    ssm_states(i + 1)
                ssm_output(i)
                if i % NBLK:
                    ssm_stats(i - 1)
                if i % NBLK == NBLK - 1:
                    ssm_stats(i)
                    act_rstd[i // NBLK] = inverse_std((i + 1 - NBLK) * TPB, (i + 1) * TPB)
                if NBLK <= i < nb - 1:
                    for f in tail[i - NBLK]:
                        f()
            ssm_memory = pg.everything_so_far()

        def channel_mixer(tag, store, before, between, weights=None):
            with ExitStack() as ph:
                xn = sb(ph, f"xnF{tag}", [P, 2, TPB, C])
                xT = sb(ph, f"xTF{tag}", [P, 2, CH, BLK + 1])
                mix = sb(ph, f"mix{tag}", [P, 2, CH, BLK])
                mix_hi = sb(ph, f"mix_hi{tag}", [P, 2, 2, CH, BLK], F32R)
                mix_lo = sb(ph, f"mix_lo{tag}", [P, 2, 2, CH, BLK], F32R)
                relu = sb(ph, f"relu{tag}", [P, CH, BLK])
                kact = sb(ph, f"kact{tag}", [P, CH, BLK])
                kact_hi = sb(ph, f"kact_hi{tag}", [P, 2, CH, BLK], F32R)
                kact_lo = sb(ph, f"kact_lo{tag}", [P, 2, CH, BLK], F32R)
                gate = sb(ph, f"gate{tag}", [P, 2, TPB, C])
                upd = sb(ph, f"upd{tag}", [P, 2, TPB, C])
                if weights is None:
                    memory = mixer_weights_memory(ph, tag)
                for e in ("sync", "tensor", "vector", "scalar", "gpsimd"):
                    need(e, before)
                if weights is None:
                    loaded = load_mixer_weights(*memory)
                xn_free, xT_free, mix_free, kact_free, gate_free, relu_free = ([None, None] for _ in range(6))
                mix_done = {(r, h): None for r in range(2) for h in range(CH)}
                stored = []
                k_parts, relu_ok, gate_ok = {}, {}, {}

                def turn(i):
                    b, j = divmod(i, NBLK)
                    s, k0 = i % 2, i * TPB
                    need("vector", seq_rstd[b], xn_free[s])
                    ready = [normalise(xn[:, s, t, :], X[:, k0 + t, :], k0 + t, "ffn_xn") for t in range(TPB)]
                    turned = transposed_tiles(k0, lambda t: xn[:, s, t, :], ready)
                    xn_free[s] = turned[-1][2]
                    if j == 0:
                        need("vector", xT_free[s])
                        edge = do("vector", "ffn_edge", lambda e: e.memset(xT[:, s, :, 0:1], 0.0))
                    else:
                        need("vector", xT_free[s], xT_state["ok"])
                        edge = do("vector", "ffn_edge", lambda e: e.tensor_copy(xT[:, s, :, 0:1], xT[:, 1 - s, :, BLK:BLK + 1]))
                    oks = []
                    for h, (n, ps, done) in enumerate(turned):
                        need("scalar", done, xT_free[s])
                        t = do("scalar", "ffn_xT", lambda e, h=h, ps=ps: e.activation(xT[:, s, h, 1:BLK + 1], ps, ACT.Copy))
                        bank_free[n] = [t]
                        oks.append(t)
                    xT_state["ok"] = oks[-1]
                    turned_ok[i] = (oks, edge)

                def mix_tokens(i):
                    s = i % 2
                    oks, edge = turned_ok[i]
                    for r in (1, 0):
                        for h in range(CH):
                            need("vector", oks[h], edge, mu_ok, mix_done[r, h])
                            t = do("vector", "mix_old", lambda e, r=r, h=h: e.tensor_scalar(
                                mix[:, r, h, :], xT[:, s, h, 0:BLK],one_mu[:, r, h:h + 1], None, ALU.mult))
                            need("vector", t)
                            t = do("vector", "mix", lambda e, r=r, h=h: e.scalar_tensor_tensor(
                                out=mix[:, r, h, :], in0=xT[:, s, h, 1:BLK + 1], scalar=mu_sb[:, r, h:h + 1],
                                in1=mix[:, r, h, :], op0=ALU.mult, op1=ALU.add))
                            xT_free[s] = t
                            need("scalar", t, mix_free[s])
                            hi = do("scalar", "mix_hi", lambda e, r=r, h=h: e.activation(mix_hi[:, s, r, h, :], mix[:, r, h, :], ACT.Copy))
                            need("gpsimd", hi, t, mix_free[s])
                            lo = do("gpsimd", "mix_lo", lambda e, r=r, h=h: e.tensor_tensor(
                                mix_lo[:, s, r, h, :], mix[:, r, h, :], mix_hi[:, s, r, h, :], ALU.subtract))
                            mix_done[r, h] = lo
                        mixed[i, r] = lo

                xT_state, turned_ok, mixed = {"ok": None}, {}, {}

                def products(i):
                    s = i % 2
                    need("tensor", mixed[i, 1], w_ok)
                    for m in range(CH):
                        n, ps = bank()
                        pairs = []
                        for c in range(CH):
                            pairs += terms((w_hi[:, 1, c, m * P:(m + 1) * P], w_lo[:, 1, c, m * P:(m + 1) * P]),
                                           (mix_hi[:, s, 1, c, :], mix_lo[:, s, 1, c, :]))
                        t = do("tensor", "ffn_k", product(ps, pairs))
                        need("scalar", t, relu_free[m])
                        relu_ok[m] = do("scalar", "ffn_relu", lambda e: e.activation(relu[:, m, :], ps, ACT.Relu))
                        bank_free[n] = [relu_ok[m]]
                    need("tensor", mixed[i, 0])
                    for t0 in range(0, TPB, 2):
                        n, ps = bank()
                        for q in range(2):
                            cols = slice((t0 + q) * P, (t0 + q + 1) * P)
                            pairs = []
                            for c in range(CH):
                                pairs += terms((mix_hi[:, s, 0, c, cols], mix_lo[:, s, 0, c, cols]),
                                               (w_hi[:, 0, c, :], w_lo[:, 0, c, :]))
                            t = do("tensor", "ffn_r", product(ps[:, q * C:(q + 1) * C], pairs))
                        need("scalar", t, gate_free[s])
                        gate_ok[i] = do("scalar", "sigmoid", lambda e: e.activation(
                            gate[:, s, t0:t0 + 2, :], ps.rearrange("p (t c) -> p t c", c=C), ACT.Sigmoid))
                        bank_free[n] = [gate_ok[i]]
                    mix_free[s] = t

                def square(i):
                    s = i % 2
                    for m in range(CH):
                        need("vector", relu_ok[m], relu_free[m])
                        t = do("vector", "ffn_square", lambda e: e.tensor_tensor(kact[:, m, :], relu[:, m, :], relu[:, m, :], ALU.mult))
                        need("vector", t, kact_free[s])
                        hi = do("vector", "kact_hi", lambda e: e.tensor_copy(kact_hi[:, s, m, :], kact[:, m, :]))
                        need("vector", hi, kact_free[s])
                        k_parts[i] = relu_free[m] = do("vector", "kact_lo", lambda e: e.tensor_tensor(
                            kact_lo[:, s, m, :], kact[:, m, :], kact_hi[:, s, m, :], ALU.subtract))

                def update(i):
                    s, k0 = i % 2, i * TPB
                    need("tensor", k_parts[i], w_ok)
                    for t0 in range(0, TPB, 2):
                        n, ps = bank()
                        for q in range(2):
                            cols = slice((t0 + q) * P, (t0 + q + 1) * P)
                            pairs = []
                            for c in range(CH):
                                pairs += terms((kact_hi[:, s, c, cols], kact_lo[:, s, c, cols]),
                                               (w_hi[:, 2, c, :], w_lo[:, 2, c, :]))
                            t = do("tensor", "ffn_v", product(ps[:, q * C:(q + 1) * C], pairs))
                        need("vector", t, gate_ok[i], gate_free[s])
                        t2 = do("vector", "gated", lambda e: e.tensor_tensor(
                            upd[:, s, t0:t0 + 2, :], ps.rearrange("p (t c) -> p t c", c=C), gate[:, s, t0:t0 + 2, :], ALU.mult))
                        bank_free[n] = [t2]
                        need("gpsimd", t2)
                        k = k0 + t0
                        X_done[k] = X_done[k + 1] = [do("gpsimd", "x_plus_ffn", lambda e: e.tensor_tensor(
                            X[:, k:k + 2, :], X[:, k:k + 2, :], upd[:, s, t0:t0 + 2, :], ALU.add))]
                    kact_free[s] = t
                    gate_free[s] = X_done[k]
                    if store:
                        need("sync", X_done[k0], X_done[k0 + TPB - 1])
                        stored.append(dma("stored", out[i * BLK:(i + 1) * BLK, :].rearrange("(t p) c -> p t c", p=P),
                                          X[:, k0:k0 + TPB, :]))

                nb = NB * NBLK
                between = between + [[]] * (nb + 1 - len(between))
                turn(0)
                w_hi, w_lo, mu_sb, one_mu, w_ok, mu_ok = weights or split_mixer_weights(*memory, *loaded)
                mix_tokens(0)
                turn(1)
                for i in range(nb + 1):
                    if i < nb:
                        products(i)
                    for f in between[i]:
                        f()
                    if i + 1 < nb:
                        mix_tokens(i + 1)
                    if i + 2 < nb:
                        turn(i + 2)
                    if i < nb:
                        square(i)
                    if i:
                        update(i - 1)
                if store:
                    need("sync", stored[-1])

        channel_mixer("a", False, ssm_memory, spread(tail_pieces(1) + stats_pieces(1, 1), NBLK - 1) + [[], []]
                      + [[f] for f in stats_pieces(0, NBLK - 1)], mixer_weights)
        tail_scope.close()

        before = pg.everything_so_far()
        with ExitStack() as ph:
            xT_hi = sb(ph, "att_xT_hi", [P, CH, T], F32R)
            xT_lo = sb(ph, "att_xT_lo", [P, CH, T], F32R)
            lat_hi = sb(ph, "lat_hi", [P, T], F32R)
            lat_lo = sb(ph, "lat_lo", [P, T], F32R)
            kd_raw = sb(ph, "kd_raw", [P, CH, RANK])
            kd_hi = sb(ph, "kd_hi", [P, CH, RANK], F32R)
            kd_lo = sb(ph, "kd_lo", [P, CH, RANK], F32R)
            w_raw = sb(ph, "wP_raw", [P, WPC])
            w_hi = [sb(ph, f"wP_hi{i}", [P, WPC], F32R) for i in range(2)]
            w_lo = [sb(ph, f"wP_lo{i}", [P, WPC], F32R) for i in range(2)]
            qA = [[sb(ph, f"qA{i}{h}", [P, BLK], F32R) for h in range(2)] for i in range(2)]
            qB = [[sb(ph, f"qB{i}{h}", [DH + 4, BLK], F32R) for h in range(2)] for i in range(2)]
            kA = [[sb(ph, f"kA{i}{h}", [P, BLK], F32R) for h in range(2)] for i in range(NK)]
            kB = [[sb(ph, f"kB{i}{h}", [DH + 4, BLK], F32R) for h in range(2)] for i in range(NK)]
            V = [sb(ph, f"V{i}", [P, TPB, P]) for i in range(NK)]
            prob = [sb(ph, f"prob{i}", [P, 2, BLK]) for i in range(NPROB)]
            xn = [sb(ph, f"att_xn{i}", [P, C]) for i in range(4)]
            acc = [sb(ph, f"acc{i}", [P, 2, BLK]) for i in range(2)]
            pick = sb(ph, "pick", [P, DSUB, QUAD // DSUB, DSUB])
            sel = acc[0]
            maskQ = sb(ph, "maskQ", [P, P], BF16)
            maskK = sb(ph, "maskK", [P, P], BF16)
            part_max = sb(ph, "part_max", [P, TPB, 2, NBLK])
            row_max = sb(ph, "row_max", [P, TPB, 2])
            neg_r = sb(ph, "neg_r", [P, TPB, 2], F32R)
            neg = sb(ph, "neg", [P, TPB, 2, 2])
            rden = sb(ph, "rden", [P, DCH])
            oT = sb(ph, "oT", [P, BLK])
            oT_hi = sb(ph, "oT_hi", [P, BLK], F32R)
            oT_lo = sb(ph, "oT_lo", [P, BLK], F32R)
            for e in ("sync", "tensor", "vector", "scalar", "gpsimd"):
                need(e, before)
            bank_free.clear()
            kd_in = dma("kd_in", kd_raw[:, :, :], wKD)
            pair0_in = dma("wP_in", w_raw[:, :], wPair[0])
            t = [do("gpsimd", "att_fill", lambda e: e.memset(pick[:, :, :, :], 0.0)),
                 do("gpsimd", "att_fill", lambda e: e.memset(sel[:, :, :], 1.0)),
                 do("gpsimd", "att_fill", lambda e: e.memset(maskQ[:, :], 0.0)),
                 do("gpsimd", "att_fill", lambda e: e.memset(maskK[:, :], 0.0))]
            need("gpsimd", t)
            for c in range(DSUB):
                do("gpsimd", "att_const", lambda e: e.memset(pick[:, c, :, c], 1.0))
            do("gpsimd", "att_const", lambda e: e.affine_select(
                out=sel[:, 0, :], in_=sel[:, 0, :], compare_op=ALU.is_ge, fill=0.0, base=DH + 1,
                pattern=[[0, BLK]], channel_multiplier=-1))
            do("gpsimd", "att_const", lambda e: e.affine_select(
                out=sel[:, 1, :], in_=sel[:, 1, :], compare_op=ALU.is_ge, fill=0.0, base=-(DH + 2),
                pattern=[[0, BLK]], channel_multiplier=1))
            do("gpsimd", "att_const", lambda e: e.affine_select(
                out=maskQ[:, :], in_=maskQ[:, :], compare_op=ALU.is_ge, fill=MASKED, base=0,
                pattern=[[-1, P]], channel_multiplier=1))
            const_ok = do("gpsimd", "att_const", lambda e: e.affine_select(
                out=maskK[:, :], in_=maskK[:, :], compare_op=ALU.is_ge, fill=MASKED, base=0,
                pattern=[[1, P]], channel_multiplier=-1))
            need("gpsimd", const_ok)
            for i in range(NK):
                for h in range(2):
                    sel_ok = do("gpsimd", "sel_rows", lambda e, i=i, h=h: e.tensor_copy(
                        kB[i][h][DH:DH + 4, :], sel[DH:DH + 4, h, :]))
            w_ok, w_free = {}, [None, None]

            def load_pair(n):
                s = n % 2
                w_ok[n] = split_weights("wP", w_raw[:, :], w_hi[s][:, :], w_lo[s][:, :], wPair[n % NPAIR],
                                        free=[w_free[s], w_ok.get(n - 1)], loaded=None if n else pair0_in)

            def wp(n, a, z):
                return (w_hi[n % 2][:, a:z], w_lo[n % 2][:, a:z])

            kv_free, q_free, prob_free = [None] * NK, [None, None], [None] * NPROB
            score_free, xn_free = [None] * NSCORE, [None, None]
            acc_free = [sel_ok, None]
            free = dict.fromkeys(("part", "neg", "rden", "oT", "xT", "lat", "out"))
            q_ok, k_ok, v_ok, m_ok, lat_ok = {}, {}, {}, {}, {}
            t_of = {"step": 0}
            units = [(b, p, j) for b in range(NB) for p in range(NPAIR) for j in range(NBLK)]

            def prepare_sequence(b):
                def normal(t):
                    need("vector", seq_rstd[b], xn_free[t // 2 % 2])
                    for k in (t, t + 1):
                        normal_ok[t] = normalise(xn[k % 4][:, :], X[:, b * NT + k, :], b * NT + k, "att_xn")

                def turn_tiles(t):
                    if t == 0:
                        normal(0)
                    if t + 2 < NT:
                        normal(t + 2)
                    n, ps = two_banks()
                    need("tensor", normal_ok[t], ident_ok)
                    for h in range(CH):
                        for q in range(2):
                            f = lambda e, h=h, q=q: e.transpose(
                                ps[:, h, q * P:(q + 1) * P], xn[(t + q) % 4][:, h * P:(h + 1) * P], ident[:, :])
                            if (h, q) != (CH - 1, 1):
                                run("tensor", f)
                    xn_free[t // 2 % 2] = done = do("tensor", "att_turned", f)
                    both, cols = ps[:, :, 0:2 * P], slice(t * P, (t + 2) * P)
                    need("scalar", done, free["xT"])
                    hi = do("scalar", "att_xT_hi", lambda e: e.activation(xT_hi[:, :, cols], both, ACT.Copy))
                    need("vector", hi, done)
                    lo = do("vector", "att_xT_lo", lambda e: e.tensor_tensor(xT_lo[:, :, cols], both, xT_hi[:, :, cols], ALU.subtract))
                    release(n, [hi, lo])
                    turned_ok[t // TPB] = lo

                def latent(j):
                    cols = slice(j * BLK, (j + 1) * BLK)
                    n, ps = one_bank()
                    need("tensor", turned_ok[j], kd_ok)
                    pairs = []
                    for c in range(CH):
                        pairs += terms((kd_hi[:, c, :], kd_lo[:, c, :]), (xT_hi[:, c, cols], xT_lo[:, c, cols]))
                    t = do("tensor", "latent", product(ps, pairs))
                    need("scalar", t, free["lat"])
                    hi = do("scalar", "lat_hi", lambda e: e.activation(lat_hi[:, cols], ps, ACT.Copy))
                    need("vector", hi, t)
                    lat_ok[b, j] = do("vector", "lat_lo", lambda e: e.tensor_tensor(lat_lo[:, cols], ps, lat_hi[:, cols], ALU.subtract))
                    release(n, [hi, lat_ok[b, j]])

                turned_ok, normal_ok = {}, {}
                return [[lambda t=t: turn_tiles(t) for t in range(j * TPB, (j + 1) * TPB, 2)] + [lambda j=j: latent(j)]
                        for j in range(NBLK)]

            def slot_of(n, j):
                return (n * NBLK + j) % NK

            def prepare(idx):
                b, p, j = units[idx]
                n = b * NPAIR + p
                qs, ks = (n * NBLK + j) % 2, slot_of(n, j)
                cols = slice(j * BLK, (j + 1) * BLK)
                u_ = (n, j)
                pieces = []

                def query():
                    need("tensor", w_ok[n], lat_ok[b, j])
                    bn, ps = one_bank()
                    pairs = []
                    for c in range(CH):
                        pairs += terms(wp(n, c * P, (c + 1) * P), (xT_hi[:, c, cols], xT_lo[:, c, cols]))
                    done = do("tensor", "q_proj", product(ps, pairs))
                    free["xT"] = done
                    readers, dup = [], []
                    for h in range(2):
                        hi_, lo_ = slice(h * DH, (h + 1) * DH), slice((1 - h) * DH, (2 - h) * DH)
                        need("scalar", done, q_free[qs])
                        hi = do("scalar", "q_hi", lambda e, h=h, hi_=hi_: e.activation(
                            qA[qs][h][hi_, :], ps[hi_, :], ACT.Copy, scale=DH ** -0.5))
                        need("vector", hi, done, q_free[qs])
                        lo = do("vector", "q_lo", lambda e, h=h, hi_=hi_, lo_=lo_: e.scalar_tensor_tensor(
                            out=qA[qs][h][lo_, :], in0=ps[hi_, :], scalar=DH ** -0.5, in1=qA[qs][h][hi_, :],
                            op0=ALU.mult, op1=ALU.subtract))
                        need("sync", hi, q_free[qs])
                        dup.append(dma(f"qB_in{qs}{h}", qB[qs][h][0:DH, :].bitcast(F32), qA[qs][h][hi_, :].bitcast(F32)))
                        readers += [hi, lo]
                    release(bn, readers)
                    q_ok[u_] = (readers, dup)

                def key():
                    bn, ps = one_bank()
                    need("tensor", w_ok[n], lat_ok[b, j])
                    done = do("tensor", "k_proj", product(ps, terms(wp(n, 2 * P, 3 * P), (lat_hi[:, cols], lat_lo[:, cols]))))
                    readers, dup = [], []
                    for h in range(2):
                        hi_, lo_ = slice(h * DH, (h + 1) * DH), slice((1 - h) * DH, (2 - h) * DH)
                        need("scalar", done, kv_free[ks])
                        hi = do("scalar", "k_hi", lambda e, h=h, hi_=hi_: e.activation(kA[ks][h][hi_, :], ps[hi_, :], ACT.Copy))
                        need("vector", hi, done, kv_free[ks])
                        lo = do("vector", "k_lo", lambda e, h=h, hi_=hi_: e.tensor_tensor(
                            kB[ks][h][0:DH, :], ps[hi_, :], kA[ks][h][hi_, :], ALU.subtract))
                        need("sync", hi, kv_free[ks])
                        dup.append(dma(f"kA_in{ks}{h}", kA[ks][h][lo_, :].bitcast(F32), kA[ks][h][hi_, :].bitcast(F32)))
                        readers += [hi, lo]
                    release(bn, readers)
                    k_ok[u_] = (readers, dup)

                def value():
                    bn, ps = one_bank()
                    need("tensor", w_ok[n], lat_ok[b, j])
                    for t in range(TPB):
                        tc = slice(j * BLK + t * P, j * BLK + (t + 1) * P)
                        last = product(ps[:, t * P:(t + 1) * P], terms((lat_hi[:, tc], lat_lo[:, tc]), wp(n, 3 * P, 4 * P)))
                        if t < TPB - 1:
                            run("tensor", last)
                    done = do("tensor", "v_proj", last)
                    free["lat"] = done
                    need("scalar", done, kv_free[ks])
                    v_ok[u_] = do("scalar", "v_out", lambda e: e.activation(
                        V[ks][:, :, :], ps.rearrange("p (t d) -> p t d", d=P), ACT.Copy))
                    release(bn, [v_ok[u_]])

                maxima = []

                def maximum(t, c):
                    bn, ps = two_banks()
                    need("tensor", q_ok[u_][0], k_ok[n, c][0], k_ok[n, c][1], const_ok)
                    diag = c == j
                    width = (t + 1) * P if diag else BLK
                    for h in range(2):
                        last = product(ps[:, h, 0:width], [(qA[qs][h][:, t * P:(t + 1) * P], kA[slot_of(n, c)][h][:, 0:width])], last=not diag)
                        if diag:
                            run("tensor", last)
                            last = lambda e: e.matmul(ps[:, h, t * P:width], ident16[:, :], maskQ[:, :], start=False, stop=True)
                        if h == 0:
                            run("tensor", last)
                    done = do("tensor", "q_dot_k", last)
                    need("vector", done, free["part"])
                    r = do("vector", "part_max", lambda e: e.reduce_max(part_max[:, t, :, c:c + 1], ps[:, :, 0:width], AX.X))
                    release(bn, [r])
                    maxima.append(r)

                neg_ok = []

                def minus_max():
                    need("vector", maxima[-1], free["neg"])
                    t = do("vector", "row_max", lambda e: e.reduce_max(row_max[:, :, :], part_max[:, :, :, 0:j + 1], AX.X))
                    free["part"] = t
                    need("vector", t)
                    t = do("vector", "neg_hi", lambda e: e.tensor_scalar(neg_r[:, :, :], row_max[:, :, :], -1.0, None, ALU.mult))
                    need("vector", t)
                    do("vector", "neg", lambda e: e.tensor_copy(neg[:, :, :, 0], neg_r[:, :, :].bitcast(F32)))
                    neg_ok.append(do("vector", "neg", lambda e: e.scalar_tensor_tensor(
                        out=neg[:, :, :, 1], in0=row_max[:, :, :], scalar=-1.0,
                        in1=neg_r[:, :, :].bitcast(F32), op0=ALU.mult, op1=ALU.subtract)))

                def turn_max():
                    bn, ps = one_bank()
                    need("tensor", neg_ok[0], ident_ok)
                    for tt in range(TPB):
                        f = lambda e: e.transpose(ps[0:4, tt * P:(tt + 1) * P],
                                                  neg[:, tt, :, :].rearrange("p a b -> p (a b)"), ident[:, :])
                        if tt < TPB - 1:
                            run("tensor", f)
                    done = do("tensor", "neg_turned", f)
                    free["neg"] = done
                    need("scalar", done, q_free[qs])
                    for h in range(2):
                        m_ok[u_] = do("scalar", "neg_rows", lambda e: e.activation(qB[qs][h][DH:DH + 4, :], ps[0:4, :], ACT.Copy))
                    release(bn, [m_ok[u_]])

                if (b, p) == (0, 0):
                    pieces = list(sequence_pieces[0][j]) if j else []
                else:
                    pieces = sum(sequence_pieces[b], []) if (p, j) == (0, 0) else []
                if (b, p, j) in STATS_BEFORE:
                    pieces += stats_pieces(STATS_BEFORE[b, p, j], NBLK)
                pieces += [key, query, value]
                for c in range(j + 1):
                    pieces += [lambda t=t, c=c: maximum(t, c) for t in range(TPB)]
                pieces += [minus_max, turn_max]
                if j == 2 and n + 1 < NB * NPAIR:
                    pieces.append(lambda: load_pair(n + 1))
                return pieces

            def finish(idx, done, total):
                b, p, j = units[idx]
                n, os_ = b * NPAIR + p, idx % 2
                st = {}

                def take_out():
                    need("scalar", done, free["oT"])
                    st["out"] = free["out"] = do("scalar", "oT_raw", lambda e: e.activation(oT[:, :], heads_out[:, :], ACT.Copy))

                def denominators():
                    bn, ps = one_bank()
                    need("tensor", total["acc"], total.get("shared"), const_ok)
                    sums = [acc[os_], acc[1 - os_]] if "shared" in total else [acc[os_]]
                    todo = [(c, i, g) for c in range(DSUB) for i in range(len(sums)) for g in range(4)]
                    for c, i, g in todo:
                        x = (g % 2 * DSUB + c) * DCH
                        f = lambda e: e.matmul(ps[g * QUAD:(g + 1) * QUAD, 0:DCH], pick[:, c, :, :].rearrange("p a b -> p (a b)"),
                                               sums[i][:, g // 2, x:x + DCH], start=(c == i == 0),
                                               stop=(c, i) == (DSUB - 1, len(sums) - 1))
                        if (c, i, g) != todo[-1]:
                            run("tensor", f)
                    t = do("tensor", "denominator", f)
                    acc_free[os_] = t
                    need("vector", t, free["rden"])
                    st["r"] = do("vector", "rden", lambda e: e.reciprocal(rden[:, :], ps[:, 0:DCH]))
                    release(bn, [st["r"]])

                def divide():
                    bn, ps = one_bank()
                    need("tensor", st["r"], ident_ok)
                    for x in range(BLK // DCH):
                        for h in range(2):
                            row = (2 * h + x // DSUB) * QUAD + x % DSUB
                            f = lambda e: e.matmul(ps[h * DH:(h + 1) * DH, x * DCH:(x + 1) * DCH],
                                                   ident[:, row:row + 1].broadcast_to([P, DH]), rden[:, :], start=True, stop=True)
                            if (x, h) != (BLK // DCH - 1, 1):
                                run("tensor", f)
                    t = free["rden"] = do("tensor", "inverses", f)
                    need("vector", t, st["out"])
                    st["o"] = do("vector", "oT", lambda e: e.tensor_tensor(oT[:, :], oT[:, :], ps, ALU.mult))
                    release(bn, [st["o"]])

                def two_parts():
                    need("scalar", st["o"], free["oT"])
                    hi = do("scalar", "oT_hi", lambda e: e.activation(oT_hi[:, :], oT[:, :], ACT.Copy))
                    need("gpsimd", hi, st["o"], free["oT"])
                    st["lo"] = do("gpsimd", "oT_lo", lambda e: e.tensor_tensor(oT_lo[:, :], oT[:, :], oT_hi[:, :], ALU.subtract))

                def project():
                    bn, ps = two_banks()
                    need("tensor", st["lo"])
                    for t in range(TPB):
                        cs = slice(t * P, (t + 1) * P)
                        y = do("tensor", "att_y", product(ps[:, t // 2, (t % 2) * C:(t % 2 + 1) * C],
                               terms((oT_hi[:, cs], oT_lo[:, cs]), wp(n, 4 * P, 4 * P + C))))
                    k = b * NT + j * TPB
                    need("vector", y, *(X_done[k + t] for t in range(TPB)))
                    x = [do("vector", "x_plus_att", lambda e: e.tensor_tensor(
                        X[:, k:k + TPB, :], X[:, k:k + TPB, :], ps[:, :, :].rearrange("p a (t c) -> p (a t) c", c=C), ALU.add))]
                    for t in range(TPB):
                        X_done[k + t] = x
                    release(bn, x)
                    free["oT"] = [y, st["lo"]]
                    w_free[n % 2] = y

                take_out()
                return [None, None, denominators, None, divide, two_parts, None, None, project]

            def weave(first, second):
                tagged = [((i + 0.5) / len(first), i, f) for i, f in enumerate(first)]
                tagged += [((i + 0.5) / len(second), i, f) for i, f in enumerate(second)]
                return [x[-1] for x in sorted(tagged, key=lambda x: x[:2])]

            sequence_pieces = [prepare_sequence(b) for b in range(NB)]
            *turns, latent0 = sequence_pieces[0][0]
            for f in turns:
                f()
            kd_ok = split_weights("kd", kd_raw[:, :, :], kd_hi[:, :, :], kd_lo[:, :, :], wKD, loaded=kd_in)
            latent0()
            load_pair(0)
            for f in prepare(0):
                f()
            def run_unit(idx, end_of_last):
                b, p, j = units[idx]
                n = b * NPAIR + p
                u_ = (n, j)
                qs = os_ = idx % 2
                nk = TPB * (j + 1)

                def score(t):
                    pr = t_of["step"] % NPROB
                    c, tt = divmod(t, TPB)
                    x0 = tt * P if c == j else 0
                    ks = slot_of(n, c)
                    kc = slice(tt * P, (tt + 1) * P)
                    for h in range(2):
                        st = (2 * t_of["step"] + h) % NSCORE
                        need("tensor", score_free[st], q_ok[u_][0], q_ok[u_][1], m_ok[u_], k_ok[n, c][0], k_ok[n, c][1], sel_ok, const_ok)
                        run("tensor", product(scores[:, st, x0:], [(kA[ks][h][:, kc], qA[qs][h][:, x0:])], last=False))
                        if c == j:
                            run("tensor", lambda e: e.matmul(scores[:, st, x0:x0 + P], ident16[:, :], maskK[:, :], start=False, stop=False))
                        done = do("tensor", "score", product(scores[:, st, x0:], [(kB[ks][h][:, kc], qB[qs][h][:, x0:])], first=False))
                        need("scalar", done, prob_free[pr])
                        score_free[st] = e_ok = do("scalar", "exp", lambda e: e.activation(prob[pr][:, h, x0:], scores[:, st, x0:], ACT.Exp))
                    t_of["step"] += 1
                    return pr, x0, e_ok

                total = {}

                def weigh(t, pr, x0, e_ok):
                    c, tt = divmod(t, TPB)
                    need("tensor", e_ok, v_ok[n, c])
                    if t == 0:
                        need("tensor", free["out"])
                    for h in range(2):
                        f = lambda e: e.matmul(heads_out[h * DH:(h + 1) * DH, x0:],
                                               V[slot_of(n, c)][:, tt, h * DH:(h + 1) * DH], prob[pr][:, h, x0:],
                                               start=(t == 0), stop=(t == nk - 1))
                        if h == 0:
                            run("tensor", f)
                    done = do("tensor", "weigh", f)
                    prob_free[pr] = [done]
                    return done

                def accumulate(t, cur, before):
                    _, pr, x0, e_ok = cur
                    if t == 0:
                        return
                    if t == 1:
                        _, pr0, _, e0 = before
                        need("gpsimd", e_ok, e0, acc_free[os_])
                        a = [do("gpsimd", "acc", lambda e: e.tensor_tensor(
                            acc[os_][:, :, x0:], prob[pr0][:, :, x0:], prob[pr][:, :, x0:], ALU.add))]
                        if x0:
                            a.append(do("gpsimd", "acc", lambda e: e.tensor_copy(acc[os_][:, :, 0:x0], prob[pr0][:, :, 0:x0])))
                        total["acc"] = a
                        prob_free[pr0].append(a[-1])
                    elif idx == len(units) - 1 and t >= nk // 2 and t % 2:
                        op = (lambda e: e.tensor_tensor(acc[1 - os_][:, :, x0:], acc[1 - os_][:, :, x0:],
                                                        prob[pr][:, :, x0:], ALU.add)) if "shared" in total else (
                            lambda e: e.tensor_copy(acc[1 - os_][:, :, :], prob[pr][:, :, :]))
                        need("vector", e_ok, total.get("shared", acc_free[1 - os_]))
                        a = total["shared"] = [do("vector", "acc_shared", op)]
                    else:
                        need("gpsimd", e_ok, total["acc"])
                        a = [do("gpsimd", "acc", lambda e: e.tensor_tensor(
                            acc[os_][:, :, x0:], acc[os_][:, :, x0:], prob[pr][:, :, x0:], ALU.add))]
                        total["acc"] = a
                    prob_free[pr].append(a[-1])

                cost = [BLK + 2 * P - max(0, t - TPB * j) * P for t in range(nk)]
                upto = [sum(cost[:t + 1]) / sum(cost) for t in range(nk)]
                fill = given = None
                prev = before = None
                for t in range(nk):
                    cur, last = (t,) + score(t), prev
                    if t == 0:
                        rest = end_of_last() if end_of_last else []
                        ahead = prepare(idx + 1) if idx + 1 < len(units) else []
                        fill, given = weave(ahead, rest), 0
                    want = min(len(fill), int(len(fill) * upto[t] / 0.95))
                    half = (given + want) // 2
                    while given < want or prev is not None:
                        if given >= half and prev is not None:
                            weigh(*prev)
                            accumulate(t - 1, prev, before)
                            prev = None
                        if given < want:
                            if fill[given]:
                                fill[given]()
                            given += 1
                    prev, before = cur, last

                def end():
                    done = weigh(*prev)
                    accumulate(nk - 1, prev, before)
                    q_free[qs] = done
                    if j == NBLK - 1:
                        for c in range(NBLK):
                            kv_free[slot_of(n, c)] = done
                    return finish(idx, done, total)

                return end

            end = None
            for idx in range(len(units)):
                end = run_unit(idx, end)
            rest = end()
            for f in rest:
                if f:
                    f()

        bank_free.clear()
        channel_mixer("b", True, pg.everything_so_far(), [[f] for f in stats_pieces(1, NBLK - 1)])


def kernel(L0_attn_a_u, L0_attn_a_A_diag, L0_attn_a_Bmat, L0_attn_a_Cmat, L0_attn_a_Dmat, L0_attn_a_h0,
           L0_attn_a_ln_gamma, L0_attn_a_ln_beta, L0_attn_b_w_kv_down, L0_attn_b_w_kv_up, L0_attn_b_w_q,
           L0_attn_b_w_out, L0_ffn_W_r, L0_ffn_W_k, L0_ffn_W_v, L0_ffn_mu_r, L0_ffn_mu_k):
    import numpy as np
    import concourse.bacc as bacc
    from concourse.bass_utils import run_bass_kernel_spmd

    def halves(w):
        return np.asarray(w).reshape(CH, P, -1).transpose(1, 0, 2)

    def cols(v):
        return np.asarray(v).reshape(CH, P).T

    wq, up, wo = np.asarray(L0_attn_b_w_q), np.asarray(L0_attn_b_w_kv_up), np.asarray(L0_attn_b_w_out)
    HD = NH * DH
    pair = [np.concatenate([halves(wq[:, i:i + P]).reshape(P, CH * P), up[:, i:i + P], up[:, HD + i:HD + i + P],
                            wo[i:i + P, :]], axis=1) for i in range(0, HD, P)]
    arrays = {
        "u": np.asarray(L0_attn_a_u).reshape(NB * T, C),
        "wA": np.stack([halves(np.asarray(w).T) for w in (L0_attn_a_Bmat, L0_attn_a_Cmat, L0_attn_a_Dmat)], axis=1),
        "wF": np.stack([halves(np.asarray(w).T) for w in (L0_ffn_W_r, L0_ffn_W_k, L0_ffn_W_v)], axis=1),
        "wKD": halves(L0_attn_b_w_kv_down),
        "wPair": np.stack(pair),
        "aDiag": cols(L0_attn_a_A_diag),
        "h0": cols(L0_attn_a_h0),
        "gb": np.broadcast_to(np.stack([np.asarray(L0_attn_a_ln_gamma), np.asarray(L0_attn_a_ln_beta)])[None], (P, 2, C)),
        "mu": np.stack([cols(L0_ffn_mu_r), cols(L0_ffn_mu_k)], axis=1),
    }
    arrays = {k: np.ascontiguousarray(v) for k, v in arrays.items()}
    nc = bacc.Bacc("TRN2", target_bir_lowering=False, num_devices=1)
    args = [nc.dram_tensor(k, v.shape, mybir.dt.from_np(v.dtype), kind="ExternalInput").ap() for k, v in arrays.items()]
    out = nc.dram_tensor("out", (NB * T, C), F32, kind="ExternalOutput").ap()
    build(nc, *args, out)
    r = run_bass_kernel_spmd(nc, [arrays], core_ids=[0])
    return r.results[0]["out"].reshape(NB, T, C)
```
